# Optimizing a Trainium2 kernel written in Bass

```python
import numpy as np
import jax
import jax.numpy as jnp

def _softmax(x, axis=-1):
    return jax.nn.softmax(x, axis=axis)

def _gelu(x):
    return jax.nn.gelu(x, approximate=True)

def _silu(x):
    return jax.nn.silu(x)

def _sigmoid(x):
    return jax.nn.sigmoid(x)

def _layernorm(x, axis=-1, eps=1e-05):
    m = jnp.mean(x, axis=axis, keepdims=True)
    v = jnp.var(x, axis=axis, keepdims=True)
    return (x - m) / jnp.sqrt(v + eps)

def _scatter_add(tgt, idx, src, axis=0):
    return tgt.at[idx].add(src)

def _segment_sum(src, seg, n):
    return jax.ops.segment_sum(src, seg, n)
kernel_name = 'mk_xattn_ffn_d2_seqx_r8_806e46'

def setup_inputs(seed: int=0):
    np.random.seed(seed)
    _w = jnp.asarray

    def _rec_inputs():
        import jax
        import jax.numpy as jnp
        _rk = jax.random.key(seed)
        x = -0.000125 + 0.9999 * jax.random.normal(jax.random.fold_in(_rk, 1), (4, 256, 256), jnp.float32)
        _lenS = 256 - jax.random.randint(jax.random.fold_in(_rk, 7), (4,), 0, max(1, 256 // 4) + 1, jnp.int32)
        _lenS2 = 256 - jax.random.randint(jax.random.fold_in(_rk, 8), (4,), 0, max(1, 256 // 4) + 1, jnp.int32)
        itok_BxS_13_99985 = jax.random.randint(jax.random.fold_in(_rk, 11), (4, 256), 13, 99986, jnp.int32)
        _ctx_2048P = jax.random.normal(jax.random.fold_in(_rk, 12), (4, 16, 256), jnp.float32)
        _ctx_2048c = jax.random.dirichlet(jax.random.fold_in(_rk, 512), 0.3 * jnp.ones((16,), jnp.float32), (4, 256))
        _ctx_2048t = jnp.einsum('bsk,bkd->bsd', _ctx_2048c, _ctx_2048P)
        _ctx_2048t = _ctx_2048t * jax.lax.rsqrt(jnp.mean(jnp.square(_ctx_2048t)) + 1e-12) * 0.953939
        ctx_2048 = 6.82029e-06 + 0.0200006 * (_ctx_2048t + 0.3 * jax.random.normal(jax.random.fold_in(_rk, 612), (4, 256, 256), jnp.float32))
        _validS = jnp.arange(256)[None, :] < _lenS[:, None]
        _validS2 = jnp.arange(256)[None, :] < _lenS2[:, None]
        _causal = jnp.tril(jnp.ones((256, 256), dtype=bool))
        mask_BxS2_bk0 = jnp.logical_not(jnp.broadcast_to(_validS2[:, :], (4, 256)))
        return (x, itok_BxS_13_99985, ctx_2048, mask_BxS2_bk0)
    x, itok_BxS_13_99985, ctx_2048, mask_BxS2_bk0 = _rec_inputs()

    def _L0_xattn_setup():
        import jax, jax.numpy as jnp
        import numpy as np
        B, S, D = (4, 512, 256)
        E = 4
        F = 1024 // E
        VOCAB = 12500
        key = jax.random.key(seed)
        k1, k2, k3, k4, k5 = jax.random.split(key, 5)
        hidden_states = jax.random.normal(k1, (B, S, D), dtype=jnp.float32)
        token_ids = jax.random.randint(k2, (B, S), 0, VOCAB, dtype=jnp.int64)
        Wg = jax.random.normal(k3, (E, F, D), dtype=jnp.float32) * 0.02
        Wu = jax.random.normal(k4, (E, F, D), dtype=jnp.float32) * 0.02
        Wd = jax.random.normal(k5, (E, D, F), dtype=jnp.float32) * 0.02
        return {'hidden_states': hidden_states, 'token_ids': token_ids, 'Wg': Wg, 'Wu': Wu, 'Wd': Wd}
    _L0_xattn_all = _L0_xattn_setup()
    _L0_xattn_in = {k: v for k, v in _L0_xattn_all.items() if k in ()}
    del _L0_xattn_all

    def _L0_ffn_setup():
        import jax, jax.numpy as jnp
        import numpy as np
        B, S, DIM = (4, 64, 256)
        E, INTER = (32, 128)
        G, TOPK_G, TOPK = (8, 4, 6)
        ROUTE_SCALE = 2.5
        SHARED_INTER = 2 * INTER

        def _gate(xf, gate_w):
            scores = jax.nn.sigmoid(xf @ gate_w.T)
            gs = scores.reshape(-1, G, E // G)
            group_scores = gs.max(axis=-1)
            _, gidx = jax.lax.top_k(group_scores, TOPK_G)
            gmask = jnp.any(jnp.arange(G)[None, None, :] == gidx[:, :, None], axis=1)
            masked = jnp.where(gmask[:, :, None], gs, -jnp.inf).reshape(-1, E)
            _, idx = jax.lax.top_k(masked, TOPK)
            w = jnp.take_along_axis(scores, idx, axis=1)
            w = w / jnp.sum(w, axis=-1, keepdims=True) * ROUTE_SCALE
            return (w, idx)
        key = jax.random.key(seed)
        ks = jax.random.split(key, 8)
        sd = 0.02
        return {'x': jax.random.normal(ks[0], (B, S, DIM), jnp.float32), 'gate_w': jax.random.normal(ks[1], (E, DIM), jnp.float32) * sd, 'w11': jax.random.normal(ks[2], (E, INTER, DIM), jnp.float32) * sd, 'w33': jax.random.normal(ks[3], (E, INTER, DIM), jnp.float32) * sd, 'w22': jax.random.normal(ks[4], (E, DIM, INTER), jnp.float32) * sd, 'sw1': jax.random.normal(ks[5], (SHARED_INTER, DIM), jnp.float32) * sd, 'sw2': jax.random.normal(ks[6], (DIM, SHARED_INTER), jnp.float32) * sd, 'sw3': jax.random.normal(ks[7], (SHARED_INTER, DIM), jnp.float32) * sd}
    _L0_ffn_all = _L0_ffn_setup()
    _L0_ffn_in = {k: v for k, v in _L0_ffn_all.items() if k in ('gate_w', 'w11', 'w33', 'w22', 'sw1', 'sw2', 'sw3')}
    del _L0_ffn_all

    def _L1_xattn_setup():
        import jax, jax.numpy as jnp
        import numpy as np
        key = jax.random.key(seed)
        k1, k2, k3 = jax.random.split(key, 3)
        B, S, D, M = (8, 256, 256, 128)
        hidden_states = jax.random.normal(k1, (B, S, D), dtype=jnp.float32)
        memory_tokens = jax.random.normal(k2, (B, M, D), dtype=jnp.float32)
        memory_mask = jax.random.randint(k3, (B, M), 0, 2).astype(jnp.bool_)
        return {'hidden_states': hidden_states, 'memory_tokens': memory_tokens, 'memory_mask': memory_mask}
    _L1_xattn_all = _L1_xattn_setup()
    _L1_xattn_in = {k: v for k, v in _L1_xattn_all.items() if k in ()}
    del _L1_xattn_all

    def _L1_ffn_setup():
        import jax, jax.numpy as jnp
        import numpy as np
        B, S, D, I, E, K = (4, 128, 256, 128, 8, 2)
        key = jax.random.key(seed)
        ks = jax.random.split(key, 7)

        def w(k, shape, fan_in):
            return jax.random.normal(k, shape, dtype=jnp.float32) * fan_in ** (-0.5)
        return {'hidden_states': jax.random.normal(ks[0], (B, S, D), dtype=jnp.float32), 'router_w': w(ks[1], (D, E), D), 'gate_up_w': w(ks[2], (E, D, 2 * I), D), 'down_w': w(ks[3], (E, I, D), I), 'shared_gate_w': w(ks[4], (D, I), D), 'shared_up_w': w(ks[5], (D, I), D), 'shared_down_w': w(ks[6], (I, D), I)}
    _L1_ffn_all = _L1_ffn_setup()
    _L1_ffn_in = {k: v for k, v in _L1_ffn_all.items() if k in ('router_w', 'gate_up_w', 'down_w', 'shared_gate_w', 'shared_up_w', 'shared_down_w')}
    del _L1_ffn_all
    return {'x': x, 'itok_BxS_13_99985': itok_BxS_13_99985, 'ctx_2048': ctx_2048, 'mask_BxS2_bk0': mask_BxS2_bk0, 'L0_ffn_gate_w': _L0_ffn_in['gate_w'], 'L0_ffn_w11': _L0_ffn_in['w11'], 'L0_ffn_w33': _L0_ffn_in['w33'], 'L0_ffn_w22': _L0_ffn_in['w22'], 'L0_ffn_sw1': _L0_ffn_in['sw1'], 'L0_ffn_sw2': _L0_ffn_in['sw2'], 'L0_ffn_sw3': _L0_ffn_in['sw3'], 'L1_ffn_router_w': _L1_ffn_in['router_w'], 'L1_ffn_gate_up_w': _L1_ffn_in['gate_up_w'], 'L1_ffn_down_w': _L1_ffn_in['down_w'], 'L1_ffn_shared_gate_w': _L1_ffn_in['shared_gate_w'], 'L1_ffn_shared_up_w': _L1_ffn_in['shared_up_w'], 'L1_ffn_shared_down_w': _L1_ffn_in['shared_down_w']}

def reference(x, itok_BxS_13_99985, ctx_2048, mask_BxS2_bk0, L0_ffn_gate_w, L0_ffn_w11, L0_ffn_w33, L0_ffn_w22, L0_ffn_sw1, L0_ffn_sw2, L0_ffn_sw3, L1_ffn_router_w, L1_ffn_gate_up_w, L1_ffn_down_w, L1_ffn_shared_gate_w, L1_ffn_shared_up_w, L1_ffn_shared_down_w):
    import jax
    import jax.numpy as jnp

    def _L0_xattn_ref(hidden_states, token_ids, Wg, Wu, Wd):
        import jax, jax.numpy as jnp
        import numpy as np
        B, S, D = (4, 512, 256)
        E = 4
        F = 1024 // E
        VOCAB = 12500
        tokens_per_expert = VOCAB // E
        tid = jnp.clip(token_ids, 0, VOCAB - 1)
        expert_ids = jnp.minimum(tid // tokens_per_expert, E - 1)
        out = jnp.zeros_like(hidden_states)
        for e in range(E):
            g = jax.nn.silu(jnp.einsum('bsd,fd->bsf', hidden_states, Wg[e]))
            u = jnp.einsum('bsd,fd->bsf', hidden_states, Wu[e])
            y = jnp.einsum('bsf,df->bsd', g * u, Wd[e])
            out = jnp.where((expert_ids == e)[..., None], y, out)
        return out

    def _L0_ffn_ref(x, gate_w, w11, w33, w22, sw1, sw2, sw3):
        import jax, jax.numpy as jnp
        import numpy as np
        B, S, DIM = (4, 64, 256)
        E, INTER = (32, 128)
        G, TOPK_G, TOPK = (8, 4, 6)
        ROUTE_SCALE = 2.5
        SHARED_INTER = 2 * INTER

        def _gate(xf, gate_w):
            scores = jax.nn.sigmoid(xf @ gate_w.T)
            gs = scores.reshape(-1, G, E // G)
            group_scores = gs.max(axis=-1)
            _, gidx = jax.lax.top_k(group_scores, TOPK_G)
            gmask = jnp.any(jnp.arange(G)[None, None, :] == gidx[:, :, None], axis=1)
            masked = jnp.where(gmask[:, :, None], gs, -jnp.inf).reshape(-1, E)
            _, idx = jax.lax.top_k(masked, TOPK)
            w = jnp.take_along_axis(scores, idx, axis=1)
            w = w / jnp.sum(w, axis=-1, keepdims=True) * ROUTE_SCALE
            return (w, idx)
        xf = x.reshape(-1, DIM)
        T = xf.shape[0]
        w, idx = _gate(xf, gate_w)
        c = jnp.zeros((T, E), xf.dtype).at[jnp.arange(T)[:, None], idx].add(w)
        g = jnp.einsum('td,eid->tei', xf, w11)
        u = jnp.einsum('td,eid->tei', xf, w33)
        act = jax.nn.silu(g) * u
        y = jnp.einsum('tei,te,edi->td', act, c, w22)
        shared = jax.nn.silu(xf @ sw1.T) * (xf @ sw3.T) @ sw2.T
        return (y + shared).reshape(x.shape)

    def _L1_xattn_ref(hidden_states, memory_tokens, memory_mask):
        import jax, jax.numpy as jnp
        import numpy as np
        B, S, D = hidden_states.shape
        scale = 1.0 / jnp.sqrt(jnp.asarray(D, hidden_states.dtype))
        scores = jnp.einsum('bsd,bmd->bsm', hidden_states, memory_tokens) * scale
        neg_inf = jnp.asarray(-1e+30, scores.dtype)
        scores = jnp.where(memory_mask[:, None, :], scores, neg_inf)
        attn = jax.nn.softmax(scores, axis=-1)
        readout = jnp.einsum('bsm,bmd->bsd', attn, memory_tokens)
        valid_b = jnp.any(memory_mask, axis=-1)
        out = jnp.where(valid_b[:, None, None], readout, jnp.zeros_like(readout))
        return out

    def _L1_ffn_ref(hidden_states, router_w, gate_up_w, down_w, shared_gate_w, shared_up_w, shared_down_w):
        import jax, jax.numpy as jnp
        import numpy as np
        B, S, D, I, E, K = (4, 128, 256, 128, 8, 2)
        Bb, Ss, Dd = hidden_states.shape
        x = hidden_states.reshape(-1, Dd)
        T = x.shape[0]
        shared = jax.nn.silu(x @ shared_gate_w) * (x @ shared_up_w) @ shared_down_w
        logits = x @ router_w
        top_val, top_idx = jax.lax.top_k(logits, K)
        probs = jnp.zeros_like(logits).at[jnp.arange(T)[:, None], top_idx].set(jax.nn.sigmoid(top_val))
        xin = probs.T[:, :, None] * x[None]
        gu = jnp.einsum('etd,edf->etf', xin, gate_up_w)
        gate, up = jnp.split(gu, 2, axis=-1)
        h = jax.nn.silu(gate) * up
        expert_out = jnp.einsum('eti,eid->etd', h, down_w)
        combined = shared + expert_out.sum(axis=0)
        return combined.reshape(Bb, Ss, Dd)
    x = x + _L0_xattn_ref(_layernorm(x, axis=-1), itok_BxS_13_99985, ctx_2048, ctx_2048, ctx_2048)
    x = x + _L0_ffn_ref(_layernorm(x, axis=-1), L0_ffn_gate_w, L0_ffn_w11, L0_ffn_w33, L0_ffn_w22, L0_ffn_sw1, L0_ffn_sw2, L0_ffn_sw3)
    x = x + _L1_xattn_ref(_layernorm(x, axis=-1), ctx_2048, mask_BxS2_bk0)
    x = x + _L1_ffn_ref(_layernorm(x, axis=-1), L1_ffn_router_w, L1_ffn_gate_up_w, L1_ffn_down_w, L1_ffn_shared_gate_w, L1_ffn_shared_up_w, L1_ffn_shared_down_w)
    return x

_drawn_inputs = setup_inputs


def setup_inputs(seed=0):
    import zlib

    import numpy as np

    out = dict(_drawn_inputs(seed))
    spreads = {}
    factors = {}
    for name, (base, spread) in spreads.items():
        noise = np.random.default_rng([zlib.crc32(name.encode()), seed]).standard_normal(out[name].shape)
        drawn = base * np.exp(spread * noise) if base else spread * noise
        out[name] = jnp.asarray(drawn.astype(out[name].dtype))
    for name, factor in factors.items():
        out[name] = (out[name] * factor).astype(out[name].dtype)
    return out
```

```python
from contextlib import ExitStack

import concourse.bass as bass
from concourse import mybir

P = 128
F32 = mybir.dt.float32
F32R = mybir.dt.float32r
I32 = mybir.dt.int32
U32 = mybir.dt.uint32
U8 = mybir.dt.uint8
ALU = mybir.AluOpType
ACT = mybir.ActivationFunctionType
AX_X = mybir.AxisListType.X
EPS = 1e-5
VOCAB = 12500
ROUTE_SCALE = 2.5
GROUPS, TOP_GROUPS, TOP_K0, TOP_K1 = 8, 4, 6, 2
MASKED = 1e30


def block_kernel(nc, x_in, tok_in, ctx_in, ctxT_in, mask_in, gate0_in, w0_in, gate1_in, w1_in, out):
    B, S, D = x_in.shape
    T = B * S
    NT = T // P
    HW = T // 2
    TH = NT // 2
    C = D // P
    M = ctx_in.shape[1]
    NEX = ctx_in.shape[0]
    FC = M // P
    U0 = w0_in.shape[0]
    U1 = w1_in.shape[0]
    E0, E1 = gate0_in.shape[2], gate1_in.shape[2]
    SH0, SH1 = U0 - E0, U1 - E1
    GU = 4 * P
    WC = GU + D
    PER_EXPERT = VOCAB // NEX
    assert HW == 512 and C == 2 and FC == 2 and U0 % 2 == 0 and SH0 == 2 and SH1 == 1

    cT_dram = [nc.dram_tensor("coef0_dram", (E0, T), F32, kind="Internal").ap(),
               nc.dram_tensor("coef1_dram", (E1, T), F32, kind="Internal").ap()]

    with ExitStack() as stack:
        def sb(name, shape, dt=F32):
            return stack.enter_context(nc.sbuf_tensor(name, shape, dt))

        def sem(name):
            return stack.enter_context(nc.semaphore(name))

        ps = stack.enter_context(nc.psum_tensor("ps", [P, 8, HW], F32))

        def gate_bank(h):
            return ps[:, 2 * h, :]

        def up_bank(h):
            return ps[:, 2 * h + 1, :]

        def y_bank(c, h):
            return ps[:, 4 + 2 * c + h, :]

        x = sb("x", [P, NT, D])
        hn = sb("hn", [P, NT, D])
        hT = sb("hT", [P, C, T])
        hT_hi = sb("hT_hi", [P, C, T], F32R)
        hT_lo = sb("hT_lo", [P, C, T], F32R)
        yT = sb("yT", [P, C, T])
        stats = sb("stats", [P, NT, 6])
        meanvar = sb("meanvar", [P, NT, 2])
        veps = sb("veps", [P, NT])
        rstd = sb("rstd", [P, NT])
        neghalf = sb("neghalf", [P, NT])
        ident = sb("ident", [P, P])
        ctx_sb = sb("ctx_sb", [P, NEX, FC, D])
        ctxT_sb = sb("ctxT_sb", [P, NEX, C, M])
        ctxT_hi = sb("ctxT_hi", [P, NEX, C, M], F32R)
        ctxT_lo = sb("ctxT_lo", [P, NEX, C, M], F32R)
        tok = sb("tok", [P, T], I32)
        tok_ge = sb("tok_ge", [P, NEX - 1, T])
        tok_mask = sb("tok_mask", [P, NEX - 1, T])
        w_raw = sb("w_raw", [P, 2, WC])
        w_hi = sb("w_hi", [P, 2, WC], F32R)
        w_lo = sb("w_lo", [P, 2, WC], F32R)
        coef = sb("coef", [P, 2, T])
        gated = sb("gated", [P, 2, HW])
        sil = sb("sil", [P, 2, HW])
        prod = sb("prod", [P, 2, HW])
        act = sb("act", [P, 2, HW])
        act_hi = sb("act_hi", [P, 2, 2, HW], F32R)
        act_lo = sb("act_lo", [P, 2, 2, HW], F32R)
        gate0 = sb("gate0", [P, C, E0])
        gate1 = sb("gate1", [P, C, E1])
        iota_i = sb("iota_i", [P, E0], I32)
        iota_f = sb("iota_f", [P, E0])
        scores = sb("scores", [P, NT, E0])
        gmax = sb("gmax", [P, NT, GROUPS])
        top_v = sb("top_v", [P, NT, 8])
        top_i = sb("top_i", [P, NT, 8], U32)
        top_f = sb("top_f", [P, NT, 8])
        g_eq = sb("g_eq", [P, NT, GROUPS, TOP_GROUPS])
        g_in = sb("g_in", [P, NT, GROUPS])
        s_in = sb("s_in", [P, NT, E0])
        s_cand = sb("s_cand", [P, NT, E0])
        w_sum = sb("w_sum", [P, NT])
        w_rec = sb("w_rec", [P, NT])
        w_top = sb("w_top", [P, NT, TOP_K0])
        e_eq = sb("e_eq", [P, NT, E0, TOP_K0])
        e_w = sb("e_w", [P, NT, E0, TOP_K0])
        ctok = sb("ctok", [P, NT, 32])
        ctrn = sb("ctrn", [P, NT, 32])
        mask_w = sb("mask_w", [P, B, M // 4], I32)
        mask_f = sb("mask_f", [P, B, M])
        mask_neg = sb("mask_neg", [P, B, M])
        valid = sb("valid", [P, B])
        sc1 = tok_ge[:, 0:2, :].rearrange("p a n -> p (a n)").rearrange("p (t m) -> p t m", m=M)
        sc2 = tok_mask[:, 0:2, :].rearrange("p a n -> p (a n)").rearrange("p (t m) -> p t m", m=M)
        negmax = sb("negmax", [P, NT])
        esum = sb("esum", [P, NT])
        erec = sb("erec", [P, NT])
        escale = sb("escale", [P, NT])
        ex = yT[:, :, :].rearrange("p c n -> p (c n)").rearrange("p (t m) -> p t m", m=M)
        exT = sb("exT", [P, NT, FC, P])

        x_loaded = [sem(f"x_loaded{h}") for h in range(2)]
        ctxT_loaded, ctx_loaded = sem("ctxT_loaded"), sem("ctx_loaded")
        tok_loaded, mask_loaded, gates_loaded = sem("tok_loaded"), sem("mask_loaded"), sem("gates_loaded")
        ident_ready, iota_ready, mask_ready = sem("ident_ready"), sem("iota_ready"), sem("mask_ready")
        zeroed, consts_done = sem("ctok_zeroed"), sem("consts_done")
        ctx_hi_done, ctx_lo_done, tok_mask_done = sem("ctx_hi_done"), sem("ctx_lo_done"), sem("tok_mask_done")
        tok_ge_done = sem("tok_ge_done")
        ones_done = sem("coef_ones_done")
        y_evac = [sem(f"y_evac{k}") for k in range(5)]
        y_turned = [sem(f"y_turned{k}") for k in range(5)]
        x_new = [sem(f"x_new{k}") for k in range(5)]
        st_done = [sem(f"st_done{k}") for k in range(4)]
        mv_done = [sem(f"mv_done{k}") for k in range(4)]
        ve_done = [sem(f"ve_done{k}") for k in range(4)]
        rs_done = [sem(f"rs_done{k}") for k in range(4)]
        h_done = [sem(f"h_done{k}") for k in range(4)]
        h_turned = [sem(f"h_turned{k}") for k in range(4)]
        hi_done = [sem(f"hT_hi_done{k}") for k in range(4)]
        lo_done = [sem(f"hT_lo_done{k}") for k in range(4)]
        hT_done = [sem(f"hT_done{k}") for k in range(4)]
        gu_done = [sem(f"gu_done{l}") for l in range(3)]
        gated_done = sem("gated_done")
        sil_done = [sem(f"sil_done{l}") for l in range(3)]
        prod_done = [sem(f"prod_done{l}") for l in range(3)]
        act_done = [sem(f"act_done{l}") for l in range(3)]
        act_hi_done = [sem(f"act_hi_done{l}") for l in range(3)]
        act_lo_done = [sem(f"act_lo_done{l}") for l in range(3)]
        down_done = [sem(f"down_done{l}") for l in range(3)]
        w_loaded = [[sem(f"w_loaded{l}_{s}") for s in range(2)] for l in range(2)]
        c_loaded = [[sem(f"c_loaded{l}_{s}") for s in range(2)] for l in range(2)]
        wgu_hi = [sem(f"wgu_hi{l}") for l in range(2)]
        wgu_lo = [sem(f"wgu_lo{l}") for l in range(2)]
        wdn_hi = [sem(f"wdn_hi{l}") for l in range(2)]
        wdn_lo = [sem(f"wdn_lo{l}") for l in range(2)]
        logits_done = [sem(f"logits_done{l}") for l in range(2)]
        scores_done = [sem(f"scores_done{l}") for l in range(2)]
        route = [sem(f"route_step{l}") for l in range(2)]
        probs_done = sem("probs_done")
        ctrn_done = [sem(f"ctrn_done{l}") for l in range(2)]
        c_stored = [sem(f"c_stored{l}") for l in range(2)]
        s_done, sc1_done, sc2_done, nm_done = sem("s_done"), sem("sc1_done"), sem("sc2_done"), sem("nm_done")
        e_done, eT_done, eT_copied, pv_done = sem("e_done"), sem("eT_done"), sem("eT_copied"), sem("pv_done")
        rec_done, escale_done = sem("rec_done"), sem("escale_done")
        stored = sem("stored")

        x_v = x_in.rearrange("b s d -> (b s) d").rearrange("(t p) d -> p t d", p=P)
        out_v = out.rearrange("b s d -> (b s) d").rearrange("(t p) d -> p t d", p=P)
        tiles_of = [range(TH * h, TH * h + TH) for h in range(2)]
        W = [w0_in, w1_in]
        UN = [U0, U1]
        SH = [SH0, SH1]
        BK = [1, 3]

        block = stack.enter_context(nc.Block())

        @block.sync
        def _(sp):
            for h in range(2):
                sp.dma_start(x[:, TH * h:TH * h + TH, :], x_v[:, TH * h:TH * h + TH, :]).then_inc(x_loaded[h], 16)
            sp.dma_start(tok[:, :], tok_in.partition_broadcast(P)).then_inc(tok_loaded, 16)
            sp.dma_start(gate0[:, :, :], gate0_in).then_inc(gates_loaded, 16)
            sp.dma_start(gate1[:, :, :], gate1_in).then_inc(gates_loaded, 16)

            def load_w(l, n, s):
                sp.dma_start(w_raw[:, s, :], W[l][n, :, :]).then_inc(w_loaded[l][s], 16)

            def load_w_again(l, n, s):
                sp.wait_ge(wgu_lo[l], n - 1)
                sp.wait_ge(wdn_lo[l], n - 1)
                load_w(l, n, s)

            def load_c(l, n, s):
                sp.wait_ge(act_done[l + 1], 2 * n - 2)
                row = cT_dram[l][n - SH[l], :]
                sp.dma_start(coef[:, s, :], row.partition_broadcast(P)).then_inc(c_loaded[l][s], 16)

            def store_c(l, E):
                sp.wait_ge(ctrn_done[l], 1)
                for q in range(4):
                    dst = cT_dram[l].rearrange("e (t q j) -> q e t j", q=4, j=32)[q, :, :, :]
                    sp.dma_start(dst, ctrn[32 * q:32 * q + E, :, :]).then_inc(c_stored[l], 16)
                sp.wait_ge(c_stored[l], 64)

            load_w(0, 0, 0)
            load_w(0, 1, 1)
            sp.dma_start(ctx_sb[:, :, :, :], ctx_in.rearrange("b (c p) d -> p b c d", p=P)).then_inc(ctx_loaded, 16)
            sp.dma_start(mask_w[:, :, :], mask_in.partition_broadcast(P)).then_inc(mask_loaded, 16)
            load_w_again(0, 2, 0)
            store_c(0, E0)
            with sp.Fori(0, (U0 - 4) // 2) as i:
                for s in range(2):
                    load_w_again(0, 2 * i + 3 + s, 1 - s)
                    load_c(0, 2 * i + 2 + s, s)
            load_w_again(0, U0 - 1, 1)
            load_c(0, U0 - 2, 0)
            load_c(0, U0 - 1, 1)
            sp.wait_ge(wgu_lo[0], U0)
            sp.wait_ge(wdn_lo[0], U0)
            load_w(1, 0, 0)
            load_w(1, 1, 1)
            load_w_again(1, 2, 0)
            store_c(1, E1)
            sp.wait_ge(act_done[1], 2 * U0)
            row = cT_dram[1][0, :]
            sp.dma_start(coef[:, 1, :], row.partition_broadcast(P)).then_inc(c_loaded[1][1], 16)
            with sp.Fori(0, (U1 - 3) // 2) as i:
                for s in range(2):
                    load_w_again(1, 2 * i + 3 + s, 1 - s)
                    load_c(1, 2 * i + 2 + s, s)
            load_c(1, U1 - 1, 0)
            for h in range(2):
                sp.wait_ge(x_new[4], TH * (h + 1))
                sp.dma_start(out_v[:, TH * h:TH * h + TH, :], x[:, TH * h:TH * h + TH, :]).then_inc(stored, 16)
            sp.wait_ge(stored, 32)

        @block.gpsimd
        def _(pool):
            pool.memset(ident[:, :], 0.0).then_inc(consts_done, 1)
            pool.memset(neghalf[:, :], -0.5).then_inc(consts_done, 1)
            pool.iota(iota_i[:, :], pattern=[[1, E0]], base=0, channel_multiplier=0).then_inc(iota_ready, 1)
            pool.wait_ge(consts_done, 2)
            pool.affine_select(out=ident[:, :], in_=ident[:, :], compare_op=ALU.not_equal, fill=1.0,
                               base=0, pattern=[[-1, P]], channel_multiplier=1).then_inc(ident_ready, 1)

            def norm(k):
                for h in range(2):
                    r = slice(TH * h, TH * h + TH)
                    pool.wait_ge(mv_done[k], TH * (h + 1))
                    pool.tensor_scalar(veps[:, r], meanvar[:, r, 1], EPS, None, ALU.add).then_inc(ve_done[k], 1)
                    pool.wait_ge(ve_done[k], h + 1)
                    pool.tensor_tensor(rstd[:, r], veps[:, r], neghalf[:, r], ALU.pow).then_inc(rs_done[k], 1)
                    pool.wait_ge(rs_done[k], h + 1)
                    for t in tiles_of[h]:
                        pool.tensor_scalar(hn[:, t, :], x[:, t, :], meanvar[:, t, 0:1], rstd[:, t:t + 1],
                                           ALU.subtract, ALU.mult).then_inc(h_done[k], 1)

            def whole_hT(k):
                for h in range(2):
                    for c in range(C):
                        pool.wait_ge(lo_done[k], 2 * h + c + 1)
                        r = slice(HW * h, HW * h + HW)
                        pool.tensor_tensor(hT[:, c, r], hT_hi[:, c, r].bitcast(F32), hT_lo[:, c, r].bitcast(F32),
                                           ALU.add).then_inc(hT_done[k], 1)

            def split_act(l, n, s, reuse):
                for h in range(2):
                    pool.wait_ge(act_hi_done[l], 2 * n + h + 1)
                    if reuse:
                        pool.wait_ge(down_done[l], 2 * n + h - 3)
                    pool.tensor_tensor(act_lo[:, s, h, :], act[:, h, :], act_hi[:, s, h, :].bitcast(F32),
                                       ALU.subtract).then_inc(act_lo_done[l], 1)

            norm(0)
            pool.wait_ge(ctx_hi_done, 1)
            pool.tensor_tensor(ctxT_lo[:, :, :, :], ctxT_sb[:, :, :, :], ctxT_hi[:, :, :, :].bitcast(F32),
                               ALU.subtract).then_inc(ctx_lo_done, 1)
            pool.wait_ge(tok_loaded, 16)
            for e in range(1, NEX):
                pool.tensor_scalar(tok_ge[:, e - 1, :], tok[:, :], float(PER_EXPERT * e), None,
                                   ALU.is_ge).then_inc(tok_ge_done, 1)
            pool.wait_ge(tok_ge_done, NEX - 1)
            pool.tensor_scalar(tok_mask[:, 0, :], tok_ge[:, 0, :], -1.0, 1.0, ALU.mult, ALU.add).then_inc(tok_mask_done, 1)
            for e in range(1, NEX - 1):
                pool.tensor_tensor(tok_mask[:, e, :], tok_ge[:, e - 1, :], tok_ge[:, e, :],
                                   ALU.subtract).then_inc(tok_mask_done, 1)
            for n in range(2 * NEX):
                split_act(0, n, n % 2, n >= 2)
            norm(1)
            whole_hT(1)
            for n in range(2):
                split_act(1, n, n, False)
            with pool.Fori(0, (U0 - 2) // 2) as i:
                for s in range(2):
                    split_act(1, 2 * i + 2 + s, s, True)
            norm(2)
            norm(3)
            whole_hT(3)
            split_act(2, 0, 0, False)
            split_act(2, 1, 1, False)
            with pool.Fori(0, (U1 - 3) // 2) as i:
                for s in range(2):
                    split_act(2, 2 * i + 2 + s, s, True)
            split_act(2, U1 - 1, 0, True)

        @block.scalar
        def _(a):
            a.dma_start(ctxT_sb[:, :, :, :], ctxT_in.rearrange("b (c p) m -> p b c m", p=P)).then_inc(ctxT_loaded, 16)
            a.wait_ge(ctxT_loaded, 16)
            a.activation(ctxT_hi[:, :, :, :], ctxT_sb[:, :, :, :], ACT.Copy).then_inc(ctx_hi_done, 1)

            def round_gate_up(l, q, s, reuse=True):
                a.wait_ge(w_loaded[l][s], 16 * q + 16)
                if reuse:
                    a.wait_ge(gu_done[l + 1], 4 * q + 2 * s - 2)
                a.activation(w_hi[:, s, 0:GU], w_raw[:, s, 0:GU], ACT.Copy).then_inc(wgu_hi[l], 1)

            def round_down(l, q, s, reuse=True):
                if reuse:
                    a.wait_ge(down_done[l + 1], 4 * q + 2 * s - 2)
                a.activation(w_hi[:, s, GU:WC], w_raw[:, s, GU:WC], ACT.Copy).then_inc(wdn_hi[l], 1)

            def turned_hi(k):
                for h in range(2):
                    a.wait_ge(h_turned[k], h + 1)
                    for c in range(C):
                        a.activation(hT_hi[:, c, HW * h:HW * h + HW], y_bank(c, h), ACT.Copy).then_inc(hi_done[k], 1)

            def evac_y(k, l, units):
                for h in range(2):
                    a.wait_ge(down_done[l], 2 * (units - 1) + h + 1)
                    for c in range(C):
                        a.activation(yT[:, c, HW * h:HW * h + HW], y_bank(c, h), ACT.Copy).then_inc(y_evac[k], 1)

            def silu(j, n, h, src, first):
                if not first:
                    a.wait_ge(prod_done[j], 2 * n + h - 1)
                a.activation(sil[:, h, :], src, ACT.Silu).then_inc(sil_done[j], 1)

            def round_act(j, n, s, h, reuse):
                a.wait_ge(act_done[j], 2 * n + h + 1)
                if reuse:
                    a.wait_ge(down_done[j], 2 * n + h - 3)
                a.activation(act_hi[:, s, h, :], act[:, h, :], ACT.Copy).then_inc(act_hi_done[j], 1)

            def step(l, q, s, first=False, reuse=True, more=True):
                n = 2 * q + s
                if not first:
                    if more:
                        round_gate_up(l, q + s, 1 - s)
                    round_down(l, q, s, reuse)
                for h in range(2):
                    if l == 1 and not first:
                        a.wait_ge(gated_done, 2 * n + h - 1)
                        silu(2, n, h, gated[:, h, :], first)
                    else:
                        a.wait_ge(gu_done[l + 1], 2 * n + h + 1)
                        silu(l + 1, n, h, gate_bank(h), first)
                for h in range(2):
                    round_act(l + 1, n, s, h, reuse)

            round_gate_up(0, 0, 0, False)
            round_down(0, 0, 0, False)
            round_gate_up(0, 0, 1, False)
            turned_hi(0)
            for n in range(2 * NEX):
                for h in range(2):
                    a.wait_ge(gu_done[0], 2 * n + h + 1)
                    silu(0, n, h, ps[:, 2 * (n % 2) + h, :], n == 0)
                for h in range(2):
                    round_act(0, n, n % 2, h, n >= 2)
            evac_y(1, 0, 2 * NEX)
            turned_hi(1)
            step(0, 0, 0, first=True, reuse=False)
            a.wait_ge(logits_done[0], 1)
            a.activation(scores[:, :, :], y_bank(1, 1)[:, 0:NT * E0].rearrange("p (t e) -> p t e", e=E0),
                         ACT.Sigmoid).then_inc(scores_done[0], 1)
            step(0, 0, 1, reuse=False)
            with a.Fori(1, U0 // 2 - 1) as q:
                for s in range(2):
                    step(0, q, s)
            step(0, U0 // 2 - 1, 0)
            step(0, U0 // 2 - 1, 1, more=False)
            evac_y(2, 1, U0)
            for h in range(2):
                a.wait_ge(h_turned[2], h + 1)
                for c in range(C):
                    a.activation(hT[:, c, HW * h:HW * h + HW], y_bank(c, h), ACT.Copy).then_inc(hT_done[2], 1)
            round_gate_up(1, 0, 0, False)
            round_down(1, 0, 0, False)
            round_gate_up(1, 0, 1, False)
            for i in range(NT + 2):
                if i < NT:
                    a.wait_ge(nm_done, i + 1)
                    a.activation(ex[:, i, :], sc2[:, i, :], ACT.Exp, bias=negmax[:, i:i + 1],
                                 accum_out=esum[:, i:i + 1]).then_inc(e_done, 1)
                if i >= 2:
                    t = i - 2
                    a.wait_ge(eT_done, t + 1)
                    a.activation(exT[:, t, :, :], ps[:, 4 + t % 2, 0:M].rearrange("p (c q) -> p c q", c=FC),
                                 ACT.Copy).then_inc(eT_copied, 1)
            turned_hi(3)
            step(1, 0, 0, first=True, reuse=False)
            a.wait_ge(logits_done[1], 1)
            a.activation(scores[:, :, 0:E1], y_bank(1, 1)[:, 0:NT * E1].rearrange("p (t e) -> p t e", e=E1),
                         ACT.Copy).then_inc(scores_done[1], 1)
            a.wait_ge(route[1], NT)
            a.activation(w_top[:, :, 0:TOP_K1], top_v[:, :, 0:TOP_K1], ACT.Sigmoid).then_inc(probs_done, 1)
            step(1, 0, 1, reuse=False)
            with a.Fori(1, U1 // 2) as q:
                for s in range(2):
                    step(1, q, s)
            step(1, U1 // 2, 0, more=False)
            evac_y(4, 2, U1)

        @block.vector
        def _(v):
            v.memset(coef[:, :, :], 1.0).then_inc(ones_done, 1)
            v.memset(ctok[:, :, :], 0.0).then_inc(zeroed, 1)

            def residual(k):
                for t in range(NT):
                    v.wait_ge(y_turned[k], t // 2 + 1)
                    v.tensor_tensor(x[:, t, :], x[:, t, :], ps[:, t // 2, D * (t % 2):D * (t % 2) + D],
                                    ALU.add).then_inc(x_new[k], 1)
                    if t % TH == TH - 1 and k < 4:
                        moments(k, t // TH)

            def moments(k, h):
                for t in tiles_of[h]:
                    if k > 0:
                        v.wait_ge(x_new[k], t + 1)
                    v.bn_stats(stats[:, t, :], x[:, t, :]).then_inc(st_done[k], 1)
                for t in tiles_of[h]:
                    v.wait_ge(st_done[k], t + 1)
                    v.bn_aggr(meanvar[:, t, :], stats[:, t, :]).then_inc(mv_done[k], 1)

            def turned_lo(k):
                for h in range(2):
                    for c in range(C):
                        v.wait_ge(hi_done[k], 2 * h + c + 1)
                        r = slice(HW * h, HW * h + HW)
                        v.tensor_tensor(hT_lo[:, c, r], y_bank(c, h), hT_hi[:, c, r].bitcast(F32),
                                        ALU.subtract).then_inc(lo_done[k], 1)

            def rest_gate_up(l, n, s):
                v.wait_ge(wgu_hi[l], n + 1)
                v.tensor_tensor(w_lo[:, s, 0:GU], w_raw[:, s, 0:GU], w_hi[:, s, 0:GU].bitcast(F32),
                                ALU.subtract).then_inc(wgu_lo[l], 1)

            def rest_down(l, n, s):
                v.wait_ge(wdn_hi[l], n + 1)
                v.tensor_tensor(w_lo[:, s, GU:WC], w_raw[:, s, GU:WC], w_hi[:, s, GU:WC].bitcast(F32),
                                ALU.subtract).then_inc(wdn_lo[l], 1)

            def times_up(l, n, h, up):
                v.wait_ge(sil_done[l], 2 * n + h + 1)
                v.tensor_tensor(prod[:, h, :], sil[:, h, :], up, ALU.mult).then_inc(prod_done[l], 1)

            def times_coef(l, n, h, c, first):
                v.wait_ge(prod_done[l], 2 * n + h + 1)
                if not first:
                    v.wait_ge(act_lo_done[l], 2 * n + h - 1)
                v.tensor_tensor(act[:, h, :], prod[:, h, :], c, ALU.mult).then_inc(act_done[l], 1)

            def step(l, q, s, first=False, routed=True, more=True):
                n = 2 * q + s
                if not first:
                    if more:
                        rest_gate_up(l, n + 1, 1 - s)
                    rest_down(l, n, s)
                if routed:
                    v.wait_ge(c_loaded[l][s], 16 * q + 16 * l * s)
                    if l == 1:
                        for h in range(2):
                            v.wait_ge(gu_done[2], 2 * n + h + 1)
                            v.tensor_tensor(gated[:, h, :], gate_bank(h), coef[:, s, HW * h:HW * h + HW],
                                            ALU.mult).then_inc(gated_done, 1)
                for h in range(2):
                    times_up(l + 1, n, h, up_bank(h))
                for h in range(2):
                    times_coef(l + 1, n, h, coef[:, s, HW * h:HW * h + HW], first)

            for h in range(2):
                v.wait_ge(x_loaded[h], 16)
                moments(0, h)
            rest_gate_up(0, 0, 0)
            rest_down(0, 0, 0)
            rest_gate_up(0, 1, 1)
            turned_lo(0)
            for n in range(2 * NEX):
                for h in range(2):
                    times_up(0, n, h, ps[:, 2 * (n % 2) + h, :])
                e = n // FC
                if e < NEX - 1:
                    v.wait_ge(tok_mask_done, e + 1)
                mask = tok_mask[:, e, :] if e < NEX - 1 else tok_ge[:, NEX - 2, :]
                for h in range(2):
                    times_coef(0, n, h, mask[:, HW * h:HW * h + HW], n == 0)
            residual(1)
            turned_lo(1)
            v.wait_ge(ones_done, 1)
            step(0, 0, 0, first=True, routed=False)

            v.wait_ge(iota_ready, 1)
            v.tensor_copy(iota_f[:, :], iota_i[:, :]).then_inc(route[0], 1)
            v.wait_ge(scores_done[0], 1)
            v.tensor_reduce(gmax[:, :, :], scores[:, :, :].rearrange("p t (g j) -> p t g j", g=GROUPS), AX_X,
                            ALU.max).then_inc(route[0], 1)
            v.wait_ge(route[0], 2)
            for t in range(NT):
                v.max(top_v[:, t, :], gmax[:, t, :]).then_inc(route[0], 1)
            for t in range(NT):
                v.wait_ge(route[0], 3 + t)
                v.max_index(top_i[:, t, :], top_v[:, t, :], gmax[:, t, :]).then_inc(route[0], 1)
            v.wait_ge(route[0], 18)
            v.tensor_copy(top_f[:, :, :], top_i[:, :, :]).then_inc(route[0], 1)
            v.wait_ge(route[0], 19)
            four = [P, NT, GROUPS, TOP_GROUPS]
            v.tensor_tensor(g_eq[:, :, :, :],
                            iota_f[:, 0:GROUPS].unsqueeze(1).unsqueeze(3).to_broadcast(four),
                            top_f[:, :, 0:TOP_GROUPS].unsqueeze(2).to_broadcast(four),
                            ALU.is_equal).then_inc(route[0], 1)
            v.wait_ge(route[0], 20)
            v.tensor_reduce(g_in[:, :, :], g_eq[:, :, :, :], AX_X, ALU.add).then_inc(route[0], 1)
            v.wait_ge(route[0], 21)
            four = [P, NT, GROUPS, E0 // GROUPS]
            sc_v = scores[:, :, :].rearrange("p t (g j) -> p t g j", g=GROUPS)
            si_v = s_in[:, :, :].rearrange("p t (g j) -> p t g j", g=GROUPS)
            ca_v = s_cand[:, :, :].rearrange("p t (g j) -> p t g j", g=GROUPS)
            v.tensor_tensor(si_v, sc_v, g_in[:, :, :].unsqueeze(3).to_broadcast(four), ALU.mult).then_inc(route[0], 1)
            v.tensor_scalar(gmax[:, :, :], g_in[:, :, :], -1.0, None, ALU.add).then_inc(route[0], 1)
            v.wait_ge(route[0], 23)
            v.tensor_tensor(ca_v, si_v, gmax[:, :, :].unsqueeze(3).to_broadcast(four), ALU.add).then_inc(route[0], 1)

            step(0, 0, 1, routed=False)

            v.wait_ge(route[0], 24)
            for t in range(NT):
                v.max(top_v[:, t, :], s_cand[:, t, :]).then_inc(route[0], 1)
            for t in range(NT):
                v.wait_ge(route[0], 25 + t)
                v.max_index(top_i[:, t, :], top_v[:, t, :], s_cand[:, t, :]).then_inc(route[0], 1)
            v.wait_ge(route[0], 40)
            v.tensor_copy(top_f[:, :, :], top_i[:, :, :]).then_inc(route[0], 1)
            v.tensor_reduce(w_sum[:, :], top_v[:, :, 0:TOP_K0], AX_X, ALU.add).then_inc(route[0], 1)
            v.wait_ge(route[0], 42)
            v.reciprocal(w_rec[:, :], w_sum[:, :]).then_inc(route[0], 1)
            four = [P, NT, E0, TOP_K0]
            v.tensor_tensor(e_eq[:, :, :, :], iota_f[:, :].unsqueeze(1).unsqueeze(3).to_broadcast(four),
                            top_f[:, :, 0:TOP_K0].unsqueeze(2).to_broadcast(four),
                            ALU.is_equal).then_inc(route[0], 1)
            v.wait_ge(route[0], 43)
            v.scalar_tensor_tensor(w_top[:, :, :], top_v[:, :, 0:TOP_K0], ROUTE_SCALE,
                                   w_rec[:, :].unsqueeze(2).to_broadcast([P, NT, TOP_K0]),
                                   ALU.mult, ALU.mult).then_inc(route[0], 1)
            v.wait_ge(route[0], 45)
            v.tensor_tensor(e_w[:, :, :, :], e_eq[:, :, :, :], w_top[:, :, :].unsqueeze(2).to_broadcast(four),
                            ALU.mult).then_inc(route[0], 1)
            v.wait_ge(route[0], 46)
            v.tensor_reduce(ctok[:, :, :], e_w[:, :, :, :], AX_X, ALU.add).then_inc(route[0], 1)
            v.wait_ge(route[0], 47)
            v.transpose(ctrn[:, :, :].rearrange("p t e -> p (t e)"),
                        ctok[:, :, :].rearrange("p t e -> p (t e)")).then_inc(ctrn_done[0], 1)

            with v.Fori(1, U0 // 2 - 1) as q:
                for s in range(2):
                    step(0, q, s)
            step(0, U0 // 2 - 1, 0)
            step(0, U0 // 2 - 1, 1, more=False)
            residual(2)
            v.wait_ge(mask_loaded, 16)
            v.tensor_copy(mask_f[:, :, :], mask_w[:, :, :].bitcast(U8)).then_inc(mask_ready, 1)
            v.wait_ge(mask_ready, 1)
            v.tensor_scalar(mask_neg[:, :, :], mask_f[:, :, :], -1.0, MASKED, ALU.add, ALU.mult).then_inc(mask_ready, 1)
            v.tensor_reduce(valid[:, :], mask_f[:, :, :], AX_X, ALU.max).then_inc(mask_ready, 1)
            v.wait_ge(mask_ready, 3)
            rest_gate_up(1, 0, 0)
            rest_down(1, 0, 0)
            rest_gate_up(1, 1, 1)
            for i in range(NT + 3):
                if i < NT:
                    b = i // (S // P)
                    v.wait_ge(s_done, i + 1)
                    v.scalar_tensor_tensor(sc1[:, i, :], ps[:, i % 4, 0:M], float(D) ** -0.5, mask_f[:, b, :],
                                           ALU.mult, ALU.mult).then_inc(sc1_done, 1)
                    v.wait_ge(sc1_done, i + 1)
                    v.tensor_tensor(sc2[:, i, :], sc1[:, i, :], mask_neg[:, b, :], ALU.add).then_inc(sc2_done, 1)
                    v.wait_ge(sc2_done, i + 1)
                    v.tensor_reduce(negmax[:, i:i + 1], sc2[:, i, :], AX_X, ALU.max, negate=True).then_inc(nm_done, 1)
                if i >= 3:
                    t = i - 3
                    b = t // (S // P)
                    v.wait_ge(e_done, t + 1)
                    v.reciprocal(erec[:, t:t + 1], esum[:, t:t + 1]).then_inc(rec_done, 1)
                    v.wait_ge(rec_done, t + 1)
                    v.tensor_tensor(escale[:, t:t + 1], erec[:, t:t + 1], valid[:, b:b + 1],
                                    ALU.mult).then_inc(escale_done, 1)
                    v.wait_ge(escale_done, t + 1)
                    v.wait_ge(pv_done, t + 1)
                    v.scalar_tensor_tensor(x[:, t, :], ps[:, 6 + t % 2, 0:D], escale[:, t:t + 1], x[:, t, :],
                                           ALU.mult, ALU.add).then_inc(x_new[3], 1)
                    if t % TH == TH - 1:
                        moments(3, t // TH)
            turned_lo(3)
            v.wait_ge(act_lo_done[1], 2 * U0)
            v.memset(coef[:, 0, :], 1.0).then_inc(ones_done, 1)
            v.wait_ge(ones_done, 2)
            v.wait_ge(c_stored[0], 64)
            v.memset(ctok[:, :, :], 0.0).then_inc(zeroed, 1)
            step(1, 0, 0, first=True, routed=False)
            v.wait_ge(scores_done[1], 1)
            for t in range(NT):
                v.max(top_v[:, t, :], scores[:, t, 0:E1]).then_inc(route[1], 1)
            v.wait_ge(route[1], NT)
            for t in range(NT):
                v.max_index(top_i[:, t, :], top_v[:, t, :], scores[:, t, 0:E1]).then_inc(route[1], 1)
            v.wait_ge(route[1], 2 * NT)
            v.tensor_copy(top_f[:, :, :], top_i[:, :, :]).then_inc(route[1], 1)
            v.wait_ge(route[1], 2 * NT + 1)
            four = [P, NT, E1, TOP_K1]
            v.tensor_tensor(e_eq[:, :, 0:E1, 0:TOP_K1], iota_f[:, 0:E1].unsqueeze(1).unsqueeze(3).to_broadcast(four),
                            top_f[:, :, 0:TOP_K1].unsqueeze(2).to_broadcast(four),
                            ALU.is_equal).then_inc(route[1], 1)
            v.wait_ge(route[1], 2 * NT + 2)
            v.wait_ge(probs_done, 1)
            v.tensor_tensor(e_w[:, :, 0:E1, 0:TOP_K1], e_eq[:, :, 0:E1, 0:TOP_K1],
                            w_top[:, :, 0:TOP_K1].unsqueeze(2).to_broadcast(four), ALU.mult).then_inc(route[1], 1)
            v.wait_ge(route[1], 2 * NT + 3)
            v.wait_ge(zeroed, 2)
            v.tensor_reduce(ctok[:, :, 0:E1], e_w[:, :, 0:E1, 0:TOP_K1], AX_X, ALU.add).then_inc(route[1], 1)
            v.wait_ge(route[1], 2 * NT + 4)
            v.transpose(ctrn[:, :, :].rearrange("p t e -> p (t e)"),
                        ctok[:, :, :].rearrange("p t e -> p (t e)")).then_inc(ctrn_done[1], 1)
            step(1, 0, 1)
            with v.Fori(1, U1 // 2) as q:
                for s in range(2):
                    step(1, q, s)
            step(1, U1 // 2, 0, more=False)
            residual(4)

        @block.tensor
        def _(pe):
            def split_product(dst, w_h, w_l, m_h, m_l, start, stop):
                pe.matmul(dst, w_h, m_h, start=start, stop=False)
                pe.matmul(dst, w_h, m_l, start=False, stop=False)
                return pe.matmul(dst, w_l, m_h, start=False, stop=stop)

            def turn_sums(k):
                for t in range(NT):
                    if t % TH == 0:
                        pe.wait_ge(y_evac[k], 2 * (t // TH + 1))
                    for c in range(C):
                        mm = pe.transpose(ps[:, t // 2, D * (t % 2) + P * c:D * (t % 2) + P * c + P],
                                          yT[:, c, P * t:P * t + P], ident[:, :])
                    if t % 2 == 1:
                        mm.then_inc(y_turned[k], 1)

            def turn_norm(k):
                for t in range(NT):
                    pe.wait_ge(h_done[k], t + 1)
                    for c in range(C):
                        mm = pe.transpose(y_bank(c, t // TH)[:, P * (t % TH):P * (t % TH) + P],
                                          hn[:, t, P * c:P * c + P], ident[:, :])
                    if t % TH == TH - 1:
                        mm.then_inc(h_turned[k], 1)

            def gate_up(l, n, s, h, first=False):
                if not first:
                    pe.wait_ge(prod_done[l + 1], 2 * n + h - 1)
                r = slice(HW * h, HW * h + HW)
                for o, dst in ((0, gate_bank(h)), (2 * P, up_bank(h))):
                    for c in range(C):
                        w = slice(o + P * c, o + P * c + P)
                        mm = split_product(dst, w_hi[:, s, w], w_lo[:, s, w], hT_hi[:, c, r], hT_lo[:, c, r],
                                           c == 0, c == C - 1)
                mm.then_inc(gu_done[l + 1], 1)

            def unit_up(l, n, s, first=False):
                pe.wait_ge(wgu_lo[l], n + 1)
                for h in range(2):
                    gate_up(l, n, s, h, first)

            def down(l, n, s, w_h, w_l, first=False, last=False):
                for h in range(2):
                    pe.wait_ge(act_lo_done[l], 2 * n + h + 1)
                    for c in range(C):
                        w = slice(P * c, P * c + P)
                        mm = split_product(y_bank(c, h), w_h[:, w], w_l[:, w], act_hi[:, s, h, :], act_lo[:, s, h, :],
                                           first, last)
                    mm.then_inc(down_done[l], 1)

            def unit_down(l, n, s, first=False, last=False):
                pe.wait_ge(wdn_lo[l], n + 1)
                down(l + 1, n, s, w_hi[:, s, GU:WC], w_lo[:, s, GU:WC], first, last)

            def logits(l, gate, E):
                pe.wait_ge(hT_done[BK[l]], 4)
                for t in range(NT):
                    for c in range(C):
                        mm = pe.matmul(y_bank(1, 1)[:, E * t:E * t + E], hT[:, c, P * t:P * t + P], gate[:, c, :],
                                       start=(c == 0), stop=(c == C - 1))
                mm.then_inc(logits_done[l], 1)

            pe.wait_ge(ident_ready, 1)
            turn_norm(0)
            pe.wait_ge(ctx_lo_done, 1)

            def hidden(n):
                e, f = n // FC, n % FC
                for h in range(2):
                    if n == 0:
                        pe.wait_ge(lo_done[0], 2 * h + 2)
                    if n >= 2:
                        pe.wait_ge(prod_done[0], 2 * (n - 2) + h + 1)
                    for c in range(C):
                        w = slice(P * f, P * f + P)
                        r = slice(HW * h, HW * h + HW)
                        mm = split_product(ps[:, 2 * (n % 2) + h, :], ctxT_hi[:, e, c, w], ctxT_lo[:, e, c, w],
                                           hT_hi[:, c, r], hT_lo[:, c, r], c == 0, c == C - 1)
                    mm.then_inc(gu_done[0], 1)

            for n in range(2 * NEX):
                hidden(n)
                if n >= 1:
                    m = n - 1
                    down(0, m, m % 2, ctxT_hi[:, m // FC, m % FC, :], ctxT_lo[:, m // FC, m % FC, :], first=(m == 0))
            m = 2 * NEX - 1
            down(0, m, m % 2, ctxT_hi[:, m // FC, m % FC, :], ctxT_lo[:, m // FC, m % FC, :], last=True)
            turn_sums(1)
            turn_norm(1)
            pe.wait_ge(wgu_lo[0], 1)
            pe.wait_ge(gates_loaded, 32)
            pe.wait_ge(lo_done[1], 2)
            gate_up(0, 0, 0, 0, first=True)
            pe.wait_ge(lo_done[1], 4)
            logits(0, gate0, E0)
            gate_up(0, 0, 0, 1, first=True)
            unit_up(0, 1, 1)
            pe.wait_ge(scores_done[0], 1)
            unit_down(0, 0, 0, first=True)
            with pe.Fori(0, (U0 - 2) // 2) as i:
                for s in range(2):
                    unit_up(0, 2 * i + 2 + s, s)
                    unit_down(0, 2 * i + 1 + s, 1 - s)
            unit_down(0, U0 - 1, 1, last=True)
            turn_sums(2)
            turn_norm(2)
            pe.wait_ge(ctx_loaded, 16)
            for i in range(NT + 3):
                if i < NT:
                    b = i // (S // P)
                    pe.wait_ge(hT_done[2], 2 * (i // TH) + 2)
                    if i >= 4:
                        pe.wait_ge(sc1_done, i - 3)
                    for c in range(C):
                        mm = pe.matmul(ps[:, i % 4, 0:M], hT[:, c, P * i:P * i + P], ctxT_sb[:, b, c, :],
                                       start=(c == 0), stop=(c == C - 1))
                    mm.then_inc(s_done, 1)
                if 2 <= i < NT + 2:
                    t = i - 2
                    if t == 0:
                        pe.wait_ge(hT_done[2], 4)
                    pe.wait_ge(e_done, t + 1)
                    if t >= 2:
                        pe.wait_ge(eT_copied, t - 1)
                    for c in range(FC):
                        mm = pe.transpose(ps[:, 4 + t % 2, P * c:P * c + P], ex[:, t, P * c:P * c + P], ident[:, :])
                    mm.then_inc(eT_done, 1)
                if i >= 3:
                    t = i - 3
                    b = t // (S // P)
                    pe.wait_ge(eT_copied, t + 1)
                    if t >= 2:
                        pe.wait_ge(x_new[3], t - 1)
                    for c in range(FC):
                        mm = pe.matmul(ps[:, 6 + t % 2, 0:D], exT[:, t, c, :], ctx_sb[:, b, c, :],
                                       start=(c == 0), stop=(c == FC - 1))
                    mm.then_inc(pv_done, 1)
            pe.wait_ge(x_new[3], NT)
            turn_norm(3)
            pe.wait_ge(wgu_lo[1], 1)
            pe.wait_ge(lo_done[3], 2)
            gate_up(1, 0, 0, 0, first=True)
            pe.wait_ge(lo_done[3], 4)
            logits(1, gate1, E1)
            gate_up(1, 0, 0, 1, first=True)
            unit_up(1, 1, 1)
            pe.wait_ge(scores_done[1], 1)
            unit_down(1, 0, 0, first=True)
            with pe.Fori(0, (U1 - 3) // 2) as i:
                for s in range(2):
                    unit_up(1, 2 * i + 2 + s, s)
                    unit_down(1, 2 * i + 1 + s, 1 - s)
            unit_up(1, U1 - 1, 0)
            unit_down(1, U1 - 2, 1)
            unit_down(1, U1 - 1, 0, last=True)
            turn_sums(4)


def kernel(x, itok_BxS_13_99985, ctx_2048, mask_BxS2_bk0, L0_ffn_gate_w, L0_ffn_w11, L0_ffn_w33, L0_ffn_w22,
           L0_ffn_sw1, L0_ffn_sw2, L0_ffn_sw3, L1_ffn_router_w, L1_ffn_gate_up_w, L1_ffn_down_w,
           L1_ffn_shared_gate_w, L1_ffn_shared_up_w, L1_ffn_shared_down_w):
    import numpy as np
    import concourse.bacc as bacc
    from concourse.bass_utils import run_bass_kernel_spmd

    def by_feature(w):
        u, d, i = w.shape
        return w.reshape(u, d // P, P, i).transpose(0, 2, 1, 3).reshape(u, P, d // P * i)

    def units(gate, up, down):
        return np.ascontiguousarray(np.concatenate([by_feature(gate), by_feature(up), down], axis=2))

    def hidden_units(w):
        return w.reshape(-1, P, w.shape[1]).transpose(0, 2, 1)

    a = {
        "x": x, "itok_BxS_13_99985": itok_BxS_13_99985, "ctx_2048": ctx_2048, "mask_BxS2_bk0": mask_BxS2_bk0,
        "L0_ffn_gate_w": L0_ffn_gate_w, "L0_ffn_w11": L0_ffn_w11, "L0_ffn_w33": L0_ffn_w33,
        "L0_ffn_w22": L0_ffn_w22, "L0_ffn_sw1": L0_ffn_sw1, "L0_ffn_sw2": L0_ffn_sw2, "L0_ffn_sw3": L0_ffn_sw3,
        "L1_ffn_router_w": L1_ffn_router_w, "L1_ffn_gate_up_w": L1_ffn_gate_up_w, "L1_ffn_down_w": L1_ffn_down_w,
        "L1_ffn_shared_gate_w": L1_ffn_shared_gate_w, "L1_ffn_shared_up_w": L1_ffn_shared_up_w,
        "L1_ffn_shared_down_w": L1_ffn_shared_down_w,
    }
    a = {k: np.asarray(v) for k, v in a.items()}
    w0 = units(np.concatenate([hidden_units(a["L0_ffn_sw1"]), a["L0_ffn_w11"].transpose(0, 2, 1)]),
               np.concatenate([hidden_units(a["L0_ffn_sw3"]), a["L0_ffn_w33"].transpose(0, 2, 1)]),
               np.concatenate([a["L0_ffn_sw2"].T.reshape(-1, P, a["L0_ffn_sw2"].shape[0]),
                               a["L0_ffn_w22"].transpose(0, 2, 1)]))
    gu, hid = a["L1_ffn_gate_up_w"], a["L1_ffn_gate_up_w"].shape[2] // 2
    w1 = units(np.concatenate([a["L1_ffn_shared_gate_w"][None], gu[:, :, :hid]]),
               np.concatenate([a["L1_ffn_shared_up_w"][None], gu[:, :, hid:]]),
               np.concatenate([a["L1_ffn_shared_down_w"][None], a["L1_ffn_down_w"]]))
    arrays = {
        "x": a["x"],
        "tok": a["itok_BxS_13_99985"].reshape(-1),
        "ctx": a["ctx_2048"],
        "ctxT": a["ctx_2048"].transpose(0, 2, 1),
        "mask": a["mask_BxS2_bk0"].view(np.int32),
        "gate0": a["L0_ffn_gate_w"].T.reshape(-1, P, a["L0_ffn_gate_w"].shape[0]).transpose(1, 0, 2),
        "w0": w0,
        "gate1": a["L1_ffn_router_w"].reshape(-1, P, a["L1_ffn_router_w"].shape[1]).transpose(1, 0, 2),
        "w1": w1,
    }
    arrays = {f"{k}_dram": np.ascontiguousarray(v) for k, v in arrays.items()}
    nc = bacc.Bacc("TRN2", target_bir_lowering=False, num_devices=1)
    args = [nc.dram_tensor(k, v.shape, mybir.dt.from_np(v.dtype), kind="ExternalInput").ap()
            for k, v in arrays.items()]
    out = nc.dram_tensor("out_dram", a["x"].shape, F32, kind="ExternalOutput").ap()
    block_kernel(nc, *args, out)
    r = run_bass_kernel_spmd(nc, [arrays], core_ids=[0])
    return r.results[0]["out_dram"]
```

```python
from contextlib import ExitStack

import concourse.bass as bass
from concourse import mybir

P = 128
F32 = mybir.dt.float32
F32R = mybir.dt.float32r
I32 = mybir.dt.int32
U32 = mybir.dt.uint32
U8 = mybir.dt.uint8
ALU = mybir.AluOpType
ACT = mybir.ActivationFunctionType
AX_X = mybir.AxisListType.X
EPS = 1e-5
VOCAB = 12500
ROUTE_SCALE = 2.5
GROUPS, TOP_GROUPS, TOP_K0, TOP_K1 = 8, 4, 6, 2
MASKED = 1e30


def block_kernel(nc, x_in, tok_in, ctx_in, ctxT_in, mask_in, gate0_in, w0_in, gate1_in, w1_in, out):
    B, S, D = x_in.shape
    T = B * S
    NT = T // P
    HW = T // 2
    TH = NT // 2
    NP = NT // 2
    C = D // P
    NEX, M = ctx_in.shape[:2]
    FC = M // P
    NA = NEX * FC
    U = [w0_in.shape[0], w1_in.shape[0]]
    E = [gate0_in.shape[2], gate1_in.shape[2]]
    SH = [U[0] - E[0], U[1] - E[1]]
    BK = [1, 3]
    GU = 4 * P
    WC = GU + D
    PER_EXPERT = VOCAB // NEX
    W = [w0_in, w1_in]
    assert HW == 512 and C == 2 and FC == 2 and S == 2 * P
    assert U[0] % 2 == 0 and U[1] % 2 == 1 and SH == [2, 1]

    cT_dram = [nc.dram_tensor(f"coef{l}_dram", (E[l], T), F32, kind="Internal").ap() for l in range(2)]

    with ExitStack() as stack:
        def sb(name, shape, dt=F32):
            return stack.enter_context(nc.sbuf_tensor(name, shape, dt))

        def sem(name):
            return stack.enter_context(nc.semaphore(name))

        ps = stack.enter_context(nc.psum_tensor("ps", [P, 8, HW], F32))

        def gate_bank(b):
            return ps[:, 2 * b, :]

        def up_bank(b):
            return ps[:, 2 * b + 1, :]

        def y_bank(c, h):
            return ps[:, 4 + 2 * c + h, :]

        def half(h):
            return slice(HW * h, HW * h + HW)

        x = sb("x", [P, NT, D])
        hn = sb("hn", [P, NT, D])
        hT = sb("hT", [P, C, T])
        hT_hi = sb("hT_hi", [P, C, T], F32R)
        hT_lo = sb("hT_lo", [P, C, T], F32R)
        yT = sb("yT", [P, C, T])
        stats = sb("stats", [P, NT, 6])
        meanvar = sb("meanvar", [P, NT, 2])
        veps = sb("veps", [P, NT])
        rstd = sb("rstd", [P, NT])
        shift = sb("shift", [P, NT])
        neghalf = sb("neghalf", [P, 2])
        warm = sb("warm", [P, 2])
        ident = sb("ident", [P, P])
        ctx_sb = sb("ctx_sb", [P, NEX, FC, D])
        ctxT_sb = sb("ctxT_sb", [P, NEX, C, M])
        ctxT_hi = sb("ctxT_hi", [P, NEX, C, M], F32R)
        ctxT_lo = sb("ctxT_lo", [P, NEX, C, M], F32R)
        tok = sb("tok", [P, T], I32)
        ge1 = sb("ge1", [P, T])
        ge2 = sb("ge2", [P, T])
        eid = sb("eid", [P, T])
        w_raw = sb("w_raw", [P, 2, WC])
        w_hi = sb("w_hi", [P, 2, WC], F32R)
        w_lo = sb("w_lo", [P, 2, WC], F32R)
        coef = sb("coef", [P, 2, T])
        gated = sb("gated", [P, 2, HW])
        sil = sb("sil", [P, 2, HW])
        prod = sb("prod", [P, 2, HW])
        act = sb("act", [P, 2, HW])
        act_hi = sb("act_hi", [P, 2, 2, HW], F32R)
        act_lo = sb("act_lo", [P, 2, 2, HW], F32R)
        gate = [sb(f"gate{l}", [P, C, E[l]]) for l in range(2)]
        iota_i = sb("iota_i", [P, E[0]], I32)
        iota_f = sb("iota_f", [P, E[0]])
        scores = sb("scores", [P, NT, E[0]])
        gmax = sb("gmax", [P, NT, GROUPS])
        top_v = sb("top_v", [P, NT, 8])
        top_i = sb("top_i", [P, NT, 8], U32)
        top_f = sb("top_f", [P, NT, 8])
        g_eq = sb("g_eq", [P, NT, GROUPS, TOP_GROUPS])
        g_in = sb("g_in", [P, NT, GROUPS])
        s_in = sb("s_in", [P, NT, E[0]])
        s_cand = sb("s_cand", [P, NT, E[0]])
        w_sum = sb("w_sum", [P, NT])
        w_rec = sb("w_rec", [P, NT])
        at_least = sb("at_least", [P, NT, E[0]])
        tied = sb("tied", [P, NT, E[0]])
        behind = sb("behind", [P, NT, E[0]])
        ctok = [sb(f"ctok{l}", [P, NT, 32]) for l in range(2)]
        ctrn = [sb(f"ctrn{l}", [P, NT, 32]) for l in range(2)]
        probs = sb("probs", [P, NT, TOP_K1])
        e_eq = sb("e_eq", [P, NT, E[1], TOP_K1])
        e_w = sb("e_w", [P, NT, E[1], TOP_K1])
        mask_w = sb("mask_w", [P, B, M // 4], I32)
        mask_f = sb("mask_f", [P, B, M])
        mask_big = sb("mask_big", [P, B, M])
        valid = sb("valid", [P, B])
        sc1 = sb("sc1", [P, NT, M])
        sc2 = sb("sc2", [P, NT, M])
        negmax = sb("negmax", [P, NT])
        esum = sb("esum", [P, NT])
        erec = sb("erec", [P, NT])
        escale = sb("escale", [P, NT])
        ex = yT[:, :, :].rearrange("p c n -> p (c n)").rearrange("p (t m) -> p t m", m=M)
        exT = sb("exT", [P, NT, FC, P])

        x_loaded = [sem(f"x_loaded{p}") for p in range(NP)]
        ctxT_loaded = [sem(f"ctxT_loaded{e}") for e in range(NEX)]
        ctx_loaded, tok_loaded = sem("ctx_loaded"), sem("tok_loaded")
        mask_loaded, gates_loaded = sem("mask_loaded"), sem("gates_loaded")
        ident_ready, iota_ready, mask_ready = sem("ident_ready"), sem("iota_ready"), sem("mask_ready")
        ident_zero, neghalf_ready, zeroed = sem("ident_zero"), sem("neghalf_ready"), sem("ctok_zeroed")
        ctx_hi_done, ctx_lo_done, ge_done = sem("ctx_hi_done"), sem("ctx_lo_done"), sem("ge_done")
        y_evac = [sem(f"y_evac{k}") for k in range(5)]
        y_turned = [sem(f"y_turned{k}") for k in range(5)]
        x_new = [sem(f"x_new{k}") for k in range(5)]
        st_done = [sem(f"st_done{k}") for k in range(4)]
        mv_done = [sem(f"mv_done{k}") for k in range(4)]
        ve_done = [sem(f"ve_done{k}") for k in range(4)]
        rs_done = [sem(f"rs_done{k}") for k in range(4)]
        sh_done = [sem(f"sh_done{k}") for k in range(4)]
        h_even = [sem(f"h_even{k}") for k in range(4)]
        h_odd = [sem(f"h_odd{k}") for k in range(4)]
        h_turned = [sem(f"h_turned{k}") for k in range(4)]
        hi_done = [sem(f"hT_hi_done{k}") for k in range(4)]
        lo_done = [sem(f"hT_lo_done{k}") for k in range(4)]
        hT_done = [sem(f"hT_done{k}") for k in range(4)]
        gu_done = [sem(f"gu_done{j}") for j in range(3)]
        sil_done = [sem(f"sil_done{j}") for j in range(3)]
        prod_done = [sem(f"prod_done{j}") for j in range(3)]
        act_done = [sem(f"act_done{j}") for j in range(3)]
        act_hi_done = [sem(f"act_hi_done{j}") for j in range(3)]
        act_lo_done = [sem(f"act_lo_done{j}") for j in range(3)]
        down_done = [sem(f"down_done{j}") for j in range(3)]
        gated_done = sem("gated_done")
        w_loaded = [[sem(f"w_loaded{l}_{s}") for s in range(2)] for l in range(2)]
        c_loaded = [[sem(f"c_loaded{l}_{s}") for s in range(2)] for l in range(2)]
        wgu_hi = [sem(f"wgu_hi{l}") for l in range(2)]
        wgu_lo = [sem(f"wgu_lo{l}") for l in range(2)]
        wdn_hi = [sem(f"wdn_hi{l}") for l in range(2)]
        wdn_lo = [sem(f"wdn_lo{l}") for l in range(2)]
        logits_done = [sem(f"logits_done{l}") for l in range(2)]
        scores_done = [sem(f"scores_done{l}") for l in range(2)]
        route = [sem(f"route_step{l}") for l in range(2)]
        probs_done = sem("probs_done")
        ctrn_done = [sem(f"ctrn_done{l}") for l in range(2)]
        c_stored = [sem(f"c_stored{l}") for l in range(2)]
        s_done, sc1_done, sc2_done = sem("s_done"), sem("sc1_done"), sem("sc2_done")
        e_done, eT_done, eT_copied, pv_done = sem("e_done"), sem("eT_done"), sem("eT_copied"), sem("pv_done")
        rec_done, escale_done = sem("rec_done"), sem("escale_done")
        stored = sem("stored")

        x_v = x_in.rearrange("b s d -> (b s) d").rearrange("(t p) d -> p t d", p=P)
        out_v = out.rearrange("b s d -> (b s) d").rearrange("(t p) d -> p t d", p=P)

        HALF_FIRST = [(0, 0), (1, 0), (0, 1), (1, 1)]
        UNIT_FIRST = [(0, 0), (0, 1), (1, 0), (1, 1)]

        block = stack.enter_context(nc.Block())

        @block.sync
        def _(sp):
            def load_x(p):
                sp.dma_start(x[:, 2 * p:2 * p + 2, :], x_v[:, 2 * p:2 * p + 2, :]).then_inc(x_loaded[p], 16)

            def load_ctxT(e):
                sp.dma_start(ctxT_sb[:, e, :, :], ctxT_in[e].rearrange("(c p) m -> p c m", p=P))\
                  .then_inc(ctxT_loaded[e], 16)

            def load_w(l, n, s):
                sp.dma_start(w_raw[:, s, :], W[l][n, :, :]).then_inc(w_loaded[l][s], 16)

            def load_w_again(l, n, s):
                sp.wait_ge(wgu_lo[l], n - 1)
                sp.wait_ge(wdn_lo[l], n - 1)
                load_w(l, n, s)

            def load_c(l, n, s):
                sp.wait_ge(act_done[l + 1], 2 * n - 2)
                sp.dma_start(coef[:, s, :], cT_dram[l][n - SH[l], :].partition_broadcast(P))\
                  .then_inc(c_loaded[l][s], 16)

            def store_c(l):
                sp.wait_ge(ctrn_done[l], 1)
                for q in range(4):
                    dst = cT_dram[l].rearrange("e (t q j) -> q e t j", q=4, j=32)[q, :, :, :]
                    sp.dma_start(dst, ctrn[l][32 * q:32 * q + E[l], :, :]).then_inc(c_stored[l], 16)
                sp.wait_ge(c_stored[l], 64)

            load_x(0)
            load_x(1)
            load_ctxT(0)
            load_x(2)
            load_x(3)
            sp.dma_start(tok[:, :], tok_in.partition_broadcast(P)).then_inc(tok_loaded, 16)
            for e in range(1, NEX):
                load_ctxT(e)
            load_w(0, 0, 0)
            load_w(0, 1, 1)
            sp.dma_start(gate[0][:, :, :], gate0_in).then_inc(gates_loaded, 16)
            sp.dma_start(gate[1][:, :, :], gate1_in).then_inc(gates_loaded, 16)
            sp.dma_start(ctx_sb[:, :, :, :], ctx_in.rearrange("b (c p) d -> p b c d", p=P)).then_inc(ctx_loaded, 16)
            sp.dma_start(mask_w[:, :, :], mask_in.partition_broadcast(P)).then_inc(mask_loaded, 16)
            load_w_again(0, 2, 0)
            store_c(0)
            load_c(0, 2, 0)
            with sp.Fori(0, (U[0] - 4) // 2) as i:
                for s in range(2):
                    load_w_again(0, 2 * i + 3 + s, 1 - s)
                    load_c(0, 2 * i + 3 + s, 1 - s)
            load_w_again(0, U[0] - 1, 1)
            load_c(0, U[0] - 1, 1)
            sp.wait_ge(wgu_lo[0], U[0])
            sp.wait_ge(wdn_lo[0], U[0])
            load_w(1, 0, 0)
            load_w(1, 1, 1)
            load_w_again(1, 2, 0)
            store_c(1)
            sp.wait_ge(act_done[1], 2 * U[0])
            sp.dma_start(coef[:, 1, :], cT_dram[1][0, :].partition_broadcast(P)).then_inc(c_loaded[1][1], 16)
            load_c(1, 2, 0)
            with sp.Fori(0, (U[1] - 3) // 2) as i:
                for s in range(2):
                    load_w_again(1, 2 * i + 3 + s, 1 - s)
                    load_c(1, 2 * i + 3 + s, 1 - s)
            for p in range(NP):
                sp.wait_ge(x_new[4], p + 1)
                sp.dma_start(out_v[:, 2 * p:2 * p + 2, :], x[:, 2 * p:2 * p + 2, :]).then_inc(stored, 16)
            sp.wait_ge(stored, 16 * NP)

        @block.gpsimd
        def _(pool):
            pool.memset(neghalf[:, :], -0.5).then_inc(neghalf_ready, 1)
            pool.memset(ident[:, :], 0.0).then_inc(ident_zero, 1)
            pool.wait_ge(ident_zero, 1)
            pool.affine_select(out=ident[:, :], in_=ident[:, :], compare_op=ALU.not_equal, fill=1.0,
                               base=0, pattern=[[-1, P]], channel_multiplier=1).then_inc(ident_ready, 1)
            pool.iota(iota_i[:, :], pattern=[[1, E[0]]], base=0, channel_multiplier=0).then_inc(iota_ready, 1)
            pool.wait_ge(neghalf_ready, 1)

            def inverse_std(k):
                for p in range(NP):
                    r = slice(2 * p, 2 * p + 2)
                    pool.wait_ge(mv_done[k], 2 * p + 2)
                    pool.tensor_scalar(veps[:, r], meanvar[:, r, 1], EPS, None, ALU.add).then_inc(ve_done[k], 1)
                    pool.wait_ge(ve_done[k], p + 1)
                    pool.tensor_tensor(rstd[:, r], veps[:, r], neghalf[:, :], ALU.pow).then_inc(rs_done[k], 1)
                    pool.wait_ge(rs_done[k], p + 1)
                    t = 2 * p + 1
                    pool.tensor_scalar(shift[:, t:t + 1], meanvar[:, t, 0:1], rstd[:, t:t + 1], -1.0,
                                       ALU.mult, ALU.mult).then_inc(sh_done[k], 1)

            def split_act(j, g, b, n, s, h, reuse):
                pool.wait_ge(act_hi_done[j], g + 1)
                if reuse:
                    pool.wait_ge(down_done[j], 2 * n + h - 3)
                pool.tensor_tensor(act_lo[:, s, h, :], act[:, b, :], act_hi[:, s, h, :].bitcast(F32),
                                   ALU.subtract).then_inc(act_lo_done[j], 1)

            inverse_std(0)
            for g in range(2 * NA):
                n, h = HALF_FIRST[g] if g < 4 else (g // 2, g % 2)
                split_act(0, g, g % 2, n, n % 2, h, n >= 2)
            inverse_std(1)
            for g, (n, h) in enumerate(HALF_FIRST):
                split_act(1, g, g % 2, n, n, h, False)
            with pool.Fori(1, U[0] // 2) as q:
                for s in range(2):
                    for h in range(2):
                        split_act(1, 4 * q + 2 * s + h, h, 2 * q + s, s, h, True)
            inverse_std(2)
            inverse_std(3)
            for g, (n, h) in enumerate(UNIT_FIRST):
                split_act(2, g, g % 2, n, n, h, False)
            with pool.Fori(1, U[1] // 2) as q:
                for s in range(2):
                    for h in range(2):
                        split_act(2, 4 * q + 2 * s + h, h, 2 * q + s, s, h, True)
            for h in range(2):
                split_act(2, 2 * U[1] - 2 + h, h, U[1] - 1, 0, h, True)

        @block.scalar
        def _(a):
            def round_gate_up(l, q, s, reuse=True):
                a.wait_ge(w_loaded[l][s], 16 * q + 16)
                if reuse:
                    a.wait_ge(gu_done[l + 1], 4 * q + 2 * s - 2)
                a.activation(w_hi[:, s, 0:GU], w_raw[:, s, 0:GU], ACT.Copy).then_inc(wgu_hi[l], 1)

            def round_down(l, q, s, reuse=True):
                if reuse:
                    a.wait_ge(down_done[l + 1], 4 * q + 2 * s - 2)
                a.activation(w_hi[:, s, GU:WC], w_raw[:, s, GU:WC], ACT.Copy).then_inc(wdn_hi[l], 1)

            def evac_y(k, j, units):
                for h in range(2):
                    a.wait_ge(down_done[j], 2 * units - 2 + 2 * h)
                    for c in range(C):
                        a.activation(yT[:, c, half(h)], y_bank(c, h), ACT.Copy).then_inc(y_evac[k], 1)

            def norm_odd(k, p):
                t = 2 * p + 1
                a.wait_ge(sh_done[k], p + 1)
                a.activation(hn[:, t, :], x[:, t, :], ACT.Identity, bias=shift[:, t:t + 1],
                             scale=rstd[:, t:t + 1]).then_inc(h_odd[k], 1)

            def turned_hi(k, h):
                a.wait_ge(h_turned[k], h + 1)
                for c in range(C):
                    a.activation(hT_hi[:, c, half(h)], y_bank(c, h), ACT.Copy).then_inc(hi_done[k], 1)

            def turned_whole(k, h):
                a.wait_ge(h_turned[k], h + 1)
                for c in range(C):
                    a.activation(hT[:, c, half(h)], y_bank(c, h), ACT.Copy).then_inc(hT_done[k], 1)

            def turned_both(k, h):
                turned_whole(k, h)
                for c in range(C):
                    a.wait_ge(hT_done[k], 2 * h + c + 1)
                    a.activation(hT_hi[:, c, half(h)], hT[:, c, half(h)], ACT.Copy).then_inc(hi_done[k], 1)

            def silu(j, g, b, src, fresh=False):
                if not fresh:
                    a.wait_ge(act_done[j], g - 1)
                a.activation(sil[:, b, :], src, ACT.Silu).then_inc(sil_done[j], 1)

            def silu_gate(j, g, b, fresh=False):
                a.wait_ge(gu_done[j], g + 1)
                silu(j, g, b, gate_bank(b), fresh)

            def silu_gated(g, b):
                a.wait_ge(gated_done, g - 2 * SH[1] + 1)
                silu(2, g, b, gated[:, b, :])

            def round_act(j, g, b, n, s, h, reuse=True):
                a.wait_ge(act_done[j], g + 1)
                if reuse:
                    a.wait_ge(down_done[j], 2 * n + h - 3)
                a.activation(act_hi[:, s, h, :], act[:, b, :], ACT.Copy).then_inc(act_hi_done[j], 1)

            def step(l, q, s, more=True):
                n = 2 * q + s
                if more:
                    round_gate_up(l, q + s, 1 - s)
                round_down(l, q, s)
                for h in range(2):
                    if l == 1:
                        silu_gated(2 * n + h, h)
                    else:
                        silu_gate(1, 2 * n + h, h)
                for h in range(2):
                    round_act(l + 1, 2 * n + h, h, n, s, h)

            def round_ctxT(e):
                a.wait_ge(ctxT_loaded[e], 16)
                a.activation(ctxT_hi[:, e, :, :], ctxT_sb[:, e, :, :], ACT.Copy).then_inc(ctx_hi_done, 1)

            a.wait_ge(neghalf_ready, 1)
            a.activation(warm[:, :], neghalf[:, :], ACT.Silu)
            norm_odd(0, 0)
            round_ctxT(0)
            norm_odd(0, 1)
            turned_hi(0, 0)
            norm_odd(0, 2)
            norm_odd(0, 3)
            turned_hi(0, 1)
            for g in range(0, 2 * NA, 2):
                for b in range(2):
                    a.wait_ge(gu_done[0], g + b + 1)
                    silu(0, g + b, b, ps[:, (g + b) % 4, :], fresh=(g == 0))
                if g % 4 == 0 and g // 4 + 1 < NEX:
                    round_ctxT(g // 4 + 1)
                for b in range(2):
                    n, h = HALF_FIRST[g + b] if g < 4 else (g // 2, b)
                    round_act(0, g + b, b, n, n % 2, h, n >= 2)
            round_gate_up(0, 0, 0, False)
            round_down(0, 0, 0, False)
            round_gate_up(0, 0, 1, False)
            evac_y(1, 0, NA)
            norm_odd(1, 0)
            norm_odd(1, 1)
            turned_both(1, 0)
            norm_odd(1, 2)
            norm_odd(1, 3)
            turned_both(1, 1)
            silu_gate(1, 0, 0, fresh=True)
            silu_gate(1, 1, 1, fresh=True)
            a.wait_ge(logits_done[0], 1)
            a.activation(scores[:, :, :], y_bank(1, 0)[:, 0:NT * E[0]].rearrange("p (t e) -> p t e", e=E[0]),
                         ACT.Sigmoid).then_inc(scores_done[0], 1)
            round_act(1, 0, 0, 0, 0, 0, False)
            round_act(1, 1, 1, 1, 1, 0, False)
            silu_gate(1, 2, 0)
            silu_gate(1, 3, 1)
            round_gate_up(0, 1, 0)
            round_down(0, 0, 1, False)
            round_act(1, 2, 0, 0, 0, 1, False)
            round_act(1, 3, 1, 1, 1, 1, False)
            with a.Fori(1, U[0] // 2 - 1) as q:
                for s in range(2):
                    step(0, q, s)
            step(0, U[0] // 2 - 1, 0)
            step(0, U[0] // 2 - 1, 1, more=False)
            evac_y(2, 1, U[0])
            norm_odd(2, 0)
            norm_odd(2, 1)
            turned_whole(2, 0)
            norm_odd(2, 2)
            norm_odd(2, 3)
            turned_whole(2, 1)
            for i in range(NT + 2):
                if i < NT:
                    a.wait_ge(sc2_done, i + 1)
                    a.activation(ex[:, i, :], sc2[:, i, :], ACT.Exp, bias=negmax[:, i:i + 1], scale=-1.0,
                                 accum_out=esum[:, i:i + 1]).then_inc(e_done, 1)
                if i >= 1 and i - 1 < NT:
                    t = i - 1
                    a.wait_ge(eT_done, t + 1)
                    a.activation(exT[:, t, :, :], ps[:, 2 + t % 2, 0:M].rearrange("p (c q) -> p c q", c=FC),
                                 ACT.Copy).then_inc(eT_copied, 1)
                if i == 1:
                    round_gate_up(1, 0, 0, False)
                    round_down(1, 0, 0, False)
                    round_gate_up(1, 0, 1, False)
                if i in (5, 7, 9):
                    norm_odd(3, (i - 5) // 2)
                if i == 8:
                    turned_both(3, 0)
            norm_odd(3, 3)
            turned_both(3, 1)
            silu_gate(2, 0, 0, fresh=True)
            a.wait_ge(logits_done[1], 1)
            a.activation(scores[:, :, 0:E[1]], y_bank(1, 0)[:, 0:NT * E[1]].rearrange("p (t e) -> p t e", e=E[1]),
                         ACT.Copy).then_inc(scores_done[1], 1)
            round_act(2, 0, 0, 0, 0, 0, False)
            a.wait_ge(route[1], NT)
            a.activation(probs[:, :, :], top_v[:, :, 0:TOP_K1], ACT.Sigmoid).then_inc(probs_done, 1)
            silu_gate(2, 1, 1, fresh=True)
            round_act(2, 1, 1, 0, 0, 1, False)
            round_gate_up(1, 1, 0)
            round_down(1, 0, 1, False)
            silu_gated(2, 0)
            silu_gated(3, 1)
            round_act(2, 2, 0, 1, 1, 0, False)
            round_act(2, 3, 1, 1, 1, 1, False)
            with a.Fori(1, U[1] // 2) as q:
                for s in range(2):
                    step(1, q, s)
            step(1, U[1] // 2, 0, more=False)
            evac_y(4, 2, U[1])

        @block.vector
        def _(v):
            v.memset(ctok[1][:, :, :], 0.0).then_inc(zeroed, 1)

            def add_pair(k, p):
                v.wait_ge(y_turned[k], p + 1)
                v.tensor_tensor(x[:, 2 * p:2 * p + 2, :], x[:, 2 * p:2 * p + 2, :],
                                ps[:, p, :].rearrange("p (t d) -> p t d", d=D), ALU.add).then_inc(x_new[k], 1)

            def moments(k, p):
                for t in (2 * p, 2 * p + 1):
                    if k == 0:
                        v.wait_ge(x_loaded[p], 16)
                    else:
                        v.wait_ge(x_new[k], t + 1 if k == 3 else p + 1)
                    v.bn_stats(stats[:, t, :], x[:, t, :]).then_inc(st_done[k], 1)
                for t in (2 * p, 2 * p + 1):
                    v.wait_ge(st_done[k], t + 1)
                    v.bn_aggr(meanvar[:, t, :], stats[:, t, :]).then_inc(mv_done[k], 1)

            def norm_even(k, p):
                t = 2 * p
                v.wait_ge(rs_done[k], p + 1)
                v.tensor_scalar(hn[:, t, :], x[:, t, :], meanvar[:, t, 0:1], rstd[:, t:t + 1],
                                ALU.subtract, ALU.mult).then_inc(h_even[k], 1)

            def turned_lo(k, h):
                for c in range(C):
                    v.wait_ge(hi_done[k], 2 * h + c + 1)
                    v.tensor_tensor(hT_lo[:, c, half(h)], y_bank(c, h) if k == 0 else hT[:, c, half(h)],
                                    hT_hi[:, c, half(h)].bitcast(F32),
                                    ALU.subtract).then_inc(lo_done[k], 1)

            def rest_gate_up(l, n, s):
                v.wait_ge(wgu_hi[l], n + 1)
                v.tensor_tensor(w_lo[:, s, 0:GU], w_raw[:, s, 0:GU], w_hi[:, s, 0:GU].bitcast(F32),
                                ALU.subtract).then_inc(wgu_lo[l], 1)

            def rest_down(l, n, s):
                v.wait_ge(wdn_hi[l], n + 1)
                v.tensor_tensor(w_lo[:, s, GU:WC], w_raw[:, s, GU:WC], w_hi[:, s, GU:WC].bitcast(F32),
                                ALU.subtract).then_inc(wdn_lo[l], 1)

            def plain(j, g, b, fresh=False):
                v.wait_ge(sil_done[j], g + 1)
                if not fresh:
                    v.wait_ge(act_lo_done[j], g - 1)
                v.tensor_tensor(act[:, b, :], sil[:, b, :], up_bank(b), ALU.mult).then_inc(act_done[j], 1)

            def times_prob(g, b, s, h):
                v.wait_ge(gu_done[2], g + 1)
                v.tensor_tensor(gated[:, b, :], gate_bank(b), coef[:, s, half(h)], ALU.mult).then_inc(gated_done, 1)

            def times_up(j, g, b, up):
                v.wait_ge(sil_done[j], g + 1)
                v.tensor_tensor(prod[:, b, :], sil[:, b, :], up, ALU.mult).then_inc(prod_done[j], 1)

            def times_coef(l, g, b, s, h):
                v.wait_ge(prod_done[l + 1], g - 2 * SH[l] + 1)
                v.wait_ge(act_lo_done[l + 1], g - 1)
                v.tensor_tensor(act[:, b, :], prod[:, b, :], coef[:, s, half(h)], ALU.mult)\
                 .then_inc(act_done[l + 1], 1)

            def unit(l, q, s, last=False):
                n = 2 * q + s
                v.wait_ge(c_loaded[l][s], 16 * q + 16 * l * s)
                if l == 1:
                    for h in range(2):
                        times_prob(2 * n + h, h, s, h)
                if last:
                    for h in range(2):
                        times_up(l + 1, 2 * n + h, h, up_bank(h))
                        times_coef(l, 2 * n + h, h, s, h)
                else:
                    for h in range(2):
                        times_up(l + 1, 2 * n + h, h, up_bank(h))
                    for h in range(2):
                        times_coef(l, 2 * n + h, h, s, h)

            def step(l, q, s, more=True):
                n = 2 * q + s
                if more:
                    rest_gate_up(l, n + 1, 1 - s)
                rest_down(l, n, s)
                unit(l, q, s, last=not more)

            def rest_ctxT(e):
                v.wait_ge(ctx_hi_done, e + 1)
                v.tensor_tensor(ctxT_lo[:, e, :, :], ctxT_sb[:, e, :, :], ctxT_hi[:, e, :, :].bitcast(F32),
                                ALU.subtract).then_inc(ctx_lo_done, 1)

            moments(0, 0)
            moments(0, 1)
            norm_even(0, 0)
            norm_even(0, 1)
            rest_ctxT(0)
            moments(0, 2)
            moments(0, 3)
            turned_lo(0, 0)
            norm_even(0, 2)
            norm_even(0, 3)
            v.wait_ge(tok_loaded, 16)
            for h in range(2):
                v.tensor_scalar(ge1[:, half(h)], tok[:, half(h)], float(PER_EXPERT), None, ALU.is_ge)\
                 .then_inc(ge_done, 1)
                if h == 1:
                    turned_lo(0, 1)
                v.wait_ge(ge_done, 3 * h + 1)
                v.scalar_tensor_tensor(ge2[:, half(h)], tok[:, half(h)], float(2 * PER_EXPERT), ge1[:, half(h)],
                                       ALU.is_ge, ALU.add).then_inc(ge_done, 1)
                v.wait_ge(ge_done, 3 * h + 2)
                v.scalar_tensor_tensor(eid[:, half(h)], tok[:, half(h)], float(3 * PER_EXPERT), ge2[:, half(h)],
                                       ALU.is_ge, ALU.add).then_inc(ge_done, 1)
            v.wait_ge(ge_done, 6)
            for g in range(2 * NA):
                b = g % 2
                n, h = HALF_FIRST[g] if g < 4 else (g // 2, b)
                times_up(0, g, b, ps[:, g % 4, :])
                if g % 4 == 1 and g // 4 + 1 < NEX:
                    rest_ctxT(g // 4 + 1)
                v.wait_ge(prod_done[0], g + 1)
                if g >= 2:
                    v.wait_ge(act_lo_done[0], g - 1)
                v.scalar_tensor_tensor(act[:, b, :], eid[:, half(h)], float(n // FC), prod[:, b, :],
                                       ALU.is_equal, ALU.mult).then_inc(act_done[0], 1)
            rest_gate_up(0, 0, 0)
            rest_down(0, 0, 0)
            rest_gate_up(0, 1, 1)

            def boundary(k, split):
                add_pair(k, 0)
                moments(k, 0)
                add_pair(k, 1)
                moments(k, 1)
                norm_even(k, 0)
                norm_even(k, 1)
                add_pair(k, 2)
                moments(k, 2)
                if split:
                    turned_lo(k, 0)
                add_pair(k, 3)
                moments(k, 3)
                norm_even(k, 2)
                norm_even(k, 3)
                if split:
                    turned_lo(k, 1)

            boundary(1, True)
            plain(1, 0, 0, fresh=True)
            plain(1, 1, 1, fresh=True)
            v.wait_ge(iota_ready, 1)
            v.tensor_copy(iota_f[:, :], iota_i[:, :]).then_inc(route[0], 1)
            v.wait_ge(scores_done[0], 1)
            v.tensor_reduce(gmax[:, :, :], scores[:, :, :].rearrange("p t (g j) -> p t g j", g=GROUPS), AX_X,
                            ALU.max).then_inc(route[0], 1)
            v.wait_ge(route[0], 2)
            for t in range(NT):
                v.max(top_v[:, t, :], gmax[:, t, :]).then_inc(route[0], 1)
            for t in range(NT):
                v.wait_ge(route[0], 3 + t)
                v.max_index(top_i[:, t, :], top_v[:, t, :], gmax[:, t, :]).then_inc(route[0], 1)
            v.wait_ge(route[0], 18)
            v.tensor_copy(top_f[:, :, :], top_i[:, :, :]).then_inc(route[0], 1)
            v.wait_ge(route[0], 19)
            four = [P, NT, GROUPS, TOP_GROUPS]
            v.tensor_tensor(g_eq[:, :, :, :],
                            iota_f[:, 0:GROUPS].unsqueeze(1).unsqueeze(3).to_broadcast(four),
                            top_f[:, :, 0:TOP_GROUPS].unsqueeze(2).to_broadcast(four),
                            ALU.is_equal).then_inc(route[0], 1)
            v.wait_ge(route[0], 20)
            v.tensor_reduce(g_in[:, :, :], g_eq[:, :, :, :], AX_X, ALU.add).then_inc(route[0], 1)
            v.wait_ge(route[0], 21)
            four = [P, NT, GROUPS, E[0] // GROUPS]
            sc_v = scores[:, :, :].rearrange("p t (g j) -> p t g j", g=GROUPS)
            si_v = s_in[:, :, :].rearrange("p t (g j) -> p t g j", g=GROUPS)
            ca_v = s_cand[:, :, :].rearrange("p t (g j) -> p t g j", g=GROUPS)
            v.tensor_tensor(si_v, sc_v, g_in[:, :, :].unsqueeze(3).to_broadcast(four), ALU.mult).then_inc(route[0], 1)
            v.tensor_scalar(gmax[:, :, :], g_in[:, :, :], -1.0, None, ALU.add).then_inc(route[0], 1)
            v.wait_ge(route[0], 23)
            v.tensor_tensor(ca_v, si_v, gmax[:, :, :].unsqueeze(3).to_broadcast(four), ALU.add).then_inc(route[0], 1)

            plain(1, 2, 0)
            rest_gate_up(0, 2, 0)
            plain(1, 3, 1)
            rest_down(0, 1, 1)

            v.wait_ge(route[0], 24)
            for t in range(NT):
                v.max(top_v[:, t, :], s_cand[:, t, :]).then_inc(route[0], 1)
            for t in range(NT):
                v.wait_ge(route[0], 25 + t)
                v.max_index(top_i[:, t, :], top_v[:, t, :], s_cand[:, t, :]).then_inc(route[0], 1)
            three = [P, NT, E[0]]
            K = TOP_K0 - 1
            v.tensor_reduce(w_sum[:, :], top_v[:, :, 0:TOP_K0], AX_X, ALU.add).then_inc(route[0], 1)
            v.tensor_tensor(at_least[:, :, :], s_cand[:, :, :], top_v[:, :, K:K + 1].to_broadcast(three),
                            ALU.is_ge).then_inc(route[0], 1)
            v.tensor_tensor(tied[:, :, :], s_cand[:, :, :], top_v[:, :, K:K + 1].to_broadcast(three),
                            ALU.is_equal).then_inc(route[0], 1)
            v.wait_ge(route[0], 41)
            v.reciprocal(w_rec[:, :], w_sum[:, :]).then_inc(route[0], 1)
            v.tensor_copy(top_f[:, :, :], top_i[:, :, :]).then_inc(route[0], 1)
            v.wait_ge(route[0], 45)
            v.tensor_tensor(behind[:, :, :], iota_f[:, :].unsqueeze(1).to_broadcast(three),
                            top_f[:, :, K:K + 1].to_broadcast(three), ALU.is_gt).then_inc(route[0], 1)
            v.scalar_tensor_tensor(s_in[:, :, :], scores[:, :, :], ROUTE_SCALE,
                                   w_rec[:, :].unsqueeze(2).to_broadcast(three), ALU.mult, ALU.mult)\
             .then_inc(route[0], 1)
            v.wait_ge(route[0], 47)
            v.tensor_tensor(tied[:, :, :], tied[:, :, :], behind[:, :, :], ALU.mult).then_inc(route[0], 1)
            v.wait_ge(route[0], 48)
            v.tensor_tensor(at_least[:, :, :], at_least[:, :, :], tied[:, :, :], ALU.subtract).then_inc(route[0], 1)
            v.wait_ge(route[0], 49)
            v.tensor_tensor(ctok[0][:, :, :], at_least[:, :, :], s_in[:, :, :], ALU.mult).then_inc(route[0], 1)
            v.wait_ge(route[0], 50)
            v.transpose(ctrn[0][:, :, :].rearrange("p t e -> p (t e)"),
                        ctok[0][:, :, :].rearrange("p t e -> p (t e)")).then_inc(ctrn_done[0], 1)

            with v.Fori(1, U[0] // 2 - 1) as q:
                for s in range(2):
                    step(0, q, s)
            step(0, U[0] // 2 - 1, 0)
            step(0, U[0] // 2 - 1, 1, more=False)
            v.wait_ge(mask_loaded, 16)
            v.tensor_copy(mask_f[:, :, :], mask_w[:, :, :].bitcast(U8)).then_inc(mask_ready, 1)
            v.wait_ge(mask_ready, 1)
            v.tensor_scalar(mask_big[:, :, :], mask_f[:, :, :], -1.0, -MASKED, ALU.add, ALU.mult).then_inc(mask_ready, 1)
            boundary(2, False)
            v.tensor_reduce(valid[:, :], mask_f[:, :, :], AX_X, ALU.max).then_inc(mask_ready, 1)
            v.wait_ge(mask_ready, 3)
            for i in range(NT + 4):
                if i < NT:
                    b = i // 2
                    v.wait_ge(s_done, i + 1)
                    v.scalar_tensor_tensor(sc1[:, i, :], ps[:, i % 2, 0:M], -float(D) ** -0.5, mask_f[:, b, :],
                                           ALU.mult, ALU.mult).then_inc(sc1_done, 1)
                    v.wait_ge(sc1_done, i + 1)
                    v.tensor_tensor_reduce(out=sc2[:, i, :], in0=sc1[:, i, :], in1=mask_big[:, b, :], scale=1.0,
                                           scalar=3e38, op0=ALU.add, op1=ALU.min,
                                           accum_out=negmax[:, i:i + 1]).then_inc(sc2_done, 1)
                if i == 2:
                    rest_gate_up(1, 0, 0)
                    rest_down(1, 0, 0)
                    rest_gate_up(1, 1, 1)
                if i >= 3 and i - 3 < NT:
                    t = i - 3
                    p = t // 2
                    if t % 2 == 0:
                        v.wait_ge(e_done, t + 2)
                        v.reciprocal(erec[:, t:t + 2], esum[:, t:t + 2]).then_inc(rec_done, 1)
                        v.wait_ge(rec_done, p + 1)
                        v.tensor_scalar(escale[:, t:t + 2], erec[:, t:t + 2], valid[:, p:p + 1], None,
                                        ALU.mult).then_inc(escale_done, 1)
                        v.wait_ge(escale_done, p + 1)
                    v.wait_ge(pv_done, t + 1)
                    v.scalar_tensor_tensor(x[:, t, :], ps[:, 5 + 2 * (t % 2), 0:D], escale[:, t:t + 1], x[:, t, :],
                                           ALU.mult, ALU.add).then_inc(x_new[3], 1)
                    if t % 2 == 1:
                        moments(3, p)
                if i in (5, 7, 9, 11):
                    norm_even(3, (i - 5) // 2)
                if i == 9:
                    turned_lo(3, 0)
            turned_lo(3, 1)
            plain(2, 0, 0, fresh=True)
            v.wait_ge(scores_done[1], 1)
            for t in range(NT):
                v.max(top_v[:, t, :], scores[:, t, 0:E[1]]).then_inc(route[1], 1)
            v.wait_ge(route[1], NT)
            for t in range(NT):
                v.max_index(top_i[:, t, :], top_v[:, t, :], scores[:, t, 0:E[1]]).then_inc(route[1], 1)
            v.wait_ge(route[1], 2 * NT)
            v.tensor_copy(top_f[:, :, :], top_i[:, :, :]).then_inc(route[1], 1)
            v.wait_ge(route[1], 2 * NT + 1)
            four = [P, NT, E[1], TOP_K1]
            v.tensor_tensor(e_eq[:, :, :, :], iota_f[:, 0:E[1]].unsqueeze(1).unsqueeze(3).to_broadcast(four),
                            top_f[:, :, 0:TOP_K1].unsqueeze(2).to_broadcast(four),
                            ALU.is_equal).then_inc(route[1], 1)
            v.wait_ge(route[1], 2 * NT + 2)
            v.wait_ge(probs_done, 1)
            v.tensor_tensor(e_w[:, :, :, :], e_eq[:, :, :, :], probs[:, :, :].unsqueeze(2).to_broadcast(four),
                            ALU.mult).then_inc(route[1], 1)
            v.wait_ge(route[1], 2 * NT + 3)
            v.wait_ge(zeroed, 1)
            v.tensor_reduce(ctok[1][:, :, 0:E[1]], e_w[:, :, :, :], AX_X, ALU.add).then_inc(route[1], 1)
            v.wait_ge(route[1], 2 * NT + 4)
            v.transpose(ctrn[1][:, :, :].rearrange("p t e -> p (t e)"),
                        ctok[1][:, :, :].rearrange("p t e -> p (t e)")).then_inc(ctrn_done[1], 1)
            plain(2, 1, 1, fresh=True)
            rest_gate_up(1, 2, 0)
            rest_down(1, 1, 1)
            unit(1, 0, 1)
            with v.Fori(1, U[1] // 2) as q:
                for s in range(2):
                    step(1, q, s)
            step(1, U[1] // 2, 0, more=False)
            for p in range(NP):
                add_pair(4, p)

        @block.tensor
        def _(pe):
            def split_product(dst, w_h, w_l, m_h, m_l, start, stop):
                pe.matmul(dst, w_h, m_h, start=start, stop=False)
                pe.matmul(dst, w_h, m_l, start=False, stop=False)
                return pe.matmul(dst, w_l, m_h, start=False, stop=stop)

            def turn_sums(k):
                for t in range(NT):
                    if t % TH == 0:
                        pe.wait_ge(y_evac[k], 2 * (t // TH + 1))
                    for c in range(C):
                        mm = pe.transpose(ps[:, t // 2, D * (t % 2) + P * c:D * (t % 2) + P * c + P],
                                          yT[:, c, P * t:P * t + P], ident[:, :])
                    if t % 2 == 1:
                        mm.then_inc(y_turned[k], 1)

            def turn_norm(k, h):
                for t in range(TH * h, TH * h + TH):
                    if t % 2 == 0:
                        pe.wait_ge(h_even[k], t // 2 + 1)
                    else:
                        pe.wait_ge(h_odd[k], t // 2 + 1)
                    for c in range(C):
                        mm = pe.transpose(y_bank(c, h)[:, P * (t % TH):P * (t % TH) + P],
                                          hn[:, t, P * c:P * c + P], ident[:, :])
                mm.then_inc(h_turned[k], 1)

            def gate_up(l, g, b, s, h, fresh=False):
                if not fresh:
                    pe.wait_ge(act_done[l + 1], g - 1)
                for o, dst in ((0, gate_bank(b)), (2 * P, up_bank(b))):
                    for c in range(C):
                        w = slice(o + P * c, o + P * c + P)
                        mm = split_product(dst, w_hi[:, s, w], w_lo[:, s, w], hT_hi[:, c, half(h)],
                                           hT_lo[:, c, half(h)], c == 0, c == C - 1)
                mm.then_inc(gu_done[l + 1], 1)

            def unit_up(l, n, s):
                pe.wait_ge(wgu_lo[l], n + 1)
                for h in range(2):
                    gate_up(l, 2 * n + h, h, s, h)

            def down(j, g, s, h, w_h, w_l, first=False, last=False):
                pe.wait_ge(act_lo_done[j], g + 1)
                for c in range(C):
                    w = slice(P * c, P * c + P)
                    mm = split_product(y_bank(c, h), w_h[:, w], w_l[:, w], act_hi[:, s, h, :], act_lo[:, s, h, :],
                                       first, last)
                mm.then_inc(down_done[j], 1)

            def unit_down(l, n, s, groups=None, first=False):
                pe.wait_ge(wdn_lo[l], n + 1)
                for h in range(2):
                    down(l + 1, 2 * n + h if groups is None else groups.index((n, h)), s, h,
                         w_hi[:, s, GU:WC], w_lo[:, s, GU:WC], first)

            def last_downs(l):
                pe.wait_ge(wdn_lo[l], U[l])
                for h in range(2):
                    for n in (U[l] - 2, U[l] - 1):
                        s = n % 2
                        down(l + 1, 2 * n + h, s, h, w_hi[:, s, GU:WC], w_lo[:, s, GU:WC], last=(n == U[l] - 1))

            def logits(l, h):
                pe.wait_ge(hT_done[BK[l]], 2 * h + 2)
                for t in range(TH * h, TH * h + TH):
                    for c in range(C):
                        mm = pe.matmul(y_bank(1, 0)[:, E[l] * t:E[l] * t + E[l]], hT[:, c, P * t:P * t + P],
                                       gate[l][:, c, :], start=(c == 0), stop=(c == C - 1))
                if h == 1:
                    mm.then_inc(logits_done[l], 1)

            pe.wait_ge(ident_ready, 1)
            turn_norm(0, 0)

            def hidden(g, n, h):
                e, f = n // FC, n % FC
                if f == 0:
                    pe.wait_ge(ctx_lo_done, e + 1)
                if g < 4:
                    pe.wait_ge(lo_done[0], 2 * h + 2)
                if g >= 4:
                    pe.wait_ge(act_done[0], g - 3)
                for c in range(C):
                    w = slice(P * f, P * f + P)
                    mm = split_product(ps[:, g % 4, :], ctxT_hi[:, e, c, w], ctxT_lo[:, e, c, w],
                                       hT_hi[:, c, half(h)], hT_lo[:, c, half(h)], c == 0, c == C - 1)
                mm.then_inc(gu_done[0], 1)

            def down_a(n, h):
                g = HALF_FIRST.index((n, h)) if n < 2 else 2 * n + h
                e, f = n // FC, n % FC
                down(0, g, n % 2, h, ctxT_hi[:, e, f, :], ctxT_lo[:, e, f, :], n == 0, n == NA - 1)

            hidden(0, 0, 0)
            hidden(1, 1, 0)
            turn_norm(0, 1)
            hidden(2, 0, 1)
            hidden(3, 1, 1)
            for n in range(2, NA):
                for h in range(2):
                    hidden(2 * n + h, n, h)
                for h in range(2):
                    down_a(n - 2, h)
            for h in range(2):
                for n in (NA - 2, NA - 1):
                    down_a(n, h)
            turn_sums(1)
            turn_norm(1, 0)
            pe.wait_ge(wgu_lo[0], 2)
            pe.wait_ge(gates_loaded, 32)
            pe.wait_ge(lo_done[1], 2)
            gate_up(0, 0, 0, 0, 0, fresh=True)
            turn_norm(1, 1)
            logits(0, 0)
            gate_up(0, 1, 1, 1, 0, fresh=True)
            logits(0, 1)
            pe.wait_ge(lo_done[1], 4)
            gate_up(0, 2, 0, 0, 1)
            gate_up(0, 3, 1, 1, 1)
            pe.wait_ge(scores_done[0], 1)
            unit_down(0, 0, 0, HALF_FIRST, first=True)
            unit_up(0, 2, 0)
            unit_down(0, 1, 1, HALF_FIRST)
            unit_up(0, 3, 1)
            unit_down(0, 2, 0)
            with pe.Fori(2, U[0] // 2 - 1) as q:
                for s in range(2):
                    unit_up(0, 2 * q + s, s)
                    unit_down(0, 2 * q - 1 + s, 1 - s)
            unit_up(0, U[0] - 2, 0)
            unit_down(0, U[0] - 3, 1)
            unit_up(0, U[0] - 1, 1)
            last_downs(0)
            turn_sums(2)
            turn_norm(2, 0)
            pe.wait_ge(ctx_loaded, 16)

            def score(t):
                pe.wait_ge(hT_done[2], 2 * (t // TH) + 2)
                if t >= 2:
                    pe.wait_ge(sc1_done, t - 1)
                for c in range(C):
                    mm = pe.matmul(ps[:, t % 2, 0:M], hT[:, c, P * t:P * t + P], ctxT_sb[:, t // 2, c, :],
                                   start=(c == 0), stop=(c == C - 1))
                mm.then_inc(s_done, 1)

            def turn_exp(t):
                pe.wait_ge(e_done, t + 1)
                if t >= 2:
                    pe.wait_ge(eT_copied, t - 1)
                for c in range(FC):
                    mm = pe.transpose(ps[:, 2 + t % 2, P * c:P * c + P], ex[:, t, P * c:P * c + P], ident[:, :])
                mm.then_inc(eT_done, 1)

            def readout(t):
                pe.wait_ge(eT_copied, t + 1)
                if t == 0:
                    pe.wait_ge(hT_done[2], 4)
                if t >= 2:
                    pe.wait_ge(x_new[3], t - 1)
                for c in range(FC):
                    mm = pe.matmul(ps[:, 5 + 2 * (t % 2), 0:D], exT[:, t, c, :], ctx_sb[:, t // 2, c, :],
                                   start=(c == 0), stop=(c == FC - 1))
                mm.then_inc(pv_done, 1)

            score(0)
            score(1)
            turn_norm(2, 1)
            for t in range(2, NT + 3):
                if t < NT:
                    score(t)
                if t - 2 < NT and t >= 2:
                    turn_exp(t - 2)
                if t >= 3:
                    readout(t - 3)
                if t == NT:
                    turn_norm(3, 0)
            pe.wait_ge(wgu_lo[1], 1)
            pe.wait_ge(lo_done[3], 2)
            gate_up(1, 0, 0, 0, 0, fresh=True)
            pe.wait_ge(x_new[3], NT)
            turn_norm(3, 1)
            logits(1, 0)
            pe.wait_ge(lo_done[3], 4)
            logits(1, 1)
            gate_up(1, 1, 1, 0, 1, fresh=True)
            unit_up(1, 1, 1)
            pe.wait_ge(scores_done[1], 1)
            unit_down(1, 0, 0, first=True)
            with pe.Fori(1, U[1] // 2) as q:
                for s in range(2):
                    unit_up(1, 2 * q + s, s)
                    unit_down(1, 2 * q - 1 + s, 1 - s)
            unit_up(1, U[1] - 1, 0)
            last_downs(1)
            turn_sums(4)


def kernel(x, itok_BxS_13_99985, ctx_2048, mask_BxS2_bk0, L0_ffn_gate_w, L0_ffn_w11, L0_ffn_w33, L0_ffn_w22,
           L0_ffn_sw1, L0_ffn_sw2, L0_ffn_sw3, L1_ffn_router_w, L1_ffn_gate_up_w, L1_ffn_down_w,
           L1_ffn_shared_gate_w, L1_ffn_shared_up_w, L1_ffn_shared_down_w):
    import numpy as np
    import concourse.bacc as bacc
    from concourse.bass_utils import run_bass_kernel_spmd

    def by_feature(w):
        u, d, i = w.shape
        return w.reshape(u, d // P, P, i).transpose(0, 2, 1, 3).reshape(u, P, d // P * i)

    def units(gate, up, down):
        return np.ascontiguousarray(np.concatenate([by_feature(gate), by_feature(up), down], axis=2))

    def hidden_units(w):
        return w.reshape(-1, P, w.shape[1]).transpose(0, 2, 1)

    a = {
        "x": x, "itok_BxS_13_99985": itok_BxS_13_99985, "ctx_2048": ctx_2048, "mask_BxS2_bk0": mask_BxS2_bk0,
        "L0_ffn_gate_w": L0_ffn_gate_w, "L0_ffn_w11": L0_ffn_w11, "L0_ffn_w33": L0_ffn_w33,
        "L0_ffn_w22": L0_ffn_w22, "L0_ffn_sw1": L0_ffn_sw1, "L0_ffn_sw2": L0_ffn_sw2, "L0_ffn_sw3": L0_ffn_sw3,
        "L1_ffn_router_w": L1_ffn_router_w, "L1_ffn_gate_up_w": L1_ffn_gate_up_w, "L1_ffn_down_w": L1_ffn_down_w,
        "L1_ffn_shared_gate_w": L1_ffn_shared_gate_w, "L1_ffn_shared_up_w": L1_ffn_shared_up_w,
        "L1_ffn_shared_down_w": L1_ffn_shared_down_w,
    }
    a = {k: np.asarray(v) for k, v in a.items()}
    w0 = units(np.concatenate([hidden_units(a["L0_ffn_sw1"]), a["L0_ffn_w11"].transpose(0, 2, 1)]),
               np.concatenate([hidden_units(a["L0_ffn_sw3"]), a["L0_ffn_w33"].transpose(0, 2, 1)]),
               np.concatenate([a["L0_ffn_sw2"].T.reshape(-1, P, a["L0_ffn_sw2"].shape[0]),
                               a["L0_ffn_w22"].transpose(0, 2, 1)]))
    gu, hid = a["L1_ffn_gate_up_w"], a["L1_ffn_gate_up_w"].shape[2] // 2
    w1 = units(np.concatenate([a["L1_ffn_shared_gate_w"][None], gu[:, :, :hid]]),
               np.concatenate([a["L1_ffn_shared_up_w"][None], gu[:, :, hid:]]),
               np.concatenate([a["L1_ffn_shared_down_w"][None], a["L1_ffn_down_w"]]))
    arrays = {
        "x": a["x"],
        "tok": a["itok_BxS_13_99985"].reshape(-1),
        "ctx": a["ctx_2048"],
        "ctxT": a["ctx_2048"].transpose(0, 2, 1),
        "mask": a["mask_BxS2_bk0"].view(np.int32),
        "gate0": a["L0_ffn_gate_w"].T.reshape(-1, P, a["L0_ffn_gate_w"].shape[0]).transpose(1, 0, 2),
        "w0": w0,
        "gate1": a["L1_ffn_router_w"].reshape(-1, P, a["L1_ffn_router_w"].shape[1]).transpose(1, 0, 2),
        "w1": w1,
    }
    arrays = {f"{k}_dram": np.ascontiguousarray(v) for k, v in arrays.items()}
    nc = bacc.Bacc("TRN2", target_bir_lowering=False, num_devices=1)
    args = [nc.dram_tensor(k, v.shape, mybir.dt.from_np(v.dtype), kind="ExternalInput").ap()
            for k, v in arrays.items()]
    out = nc.dram_tensor("out_dram", a["x"].shape, F32, kind="ExternalOutput").ap()
    block_kernel(nc, *args, out)
    r = run_bass_kernel_spmd(nc, [arrays], core_ids=[0])
    return r.results[0]["out_dram"]
```

```python
from contextlib import ExitStack

import concourse.bass as bass
from concourse import mybir

P = 128
F32 = mybir.dt.float32
F32R = mybir.dt.float32r
I32 = mybir.dt.int32
U32 = mybir.dt.uint32
U8 = mybir.dt.uint8
ALU = mybir.AluOpType
ACT = mybir.ActivationFunctionType
AX_X = mybir.AxisListType.X
EPS = 1e-5
VOCAB = 12500
ROUTE_SCALE = 2.5
GROUPS, TOP_GROUPS, TOP_K0, TOP_K1 = 8, 4, 6, 2
MASKED = 1e30


def block_kernel(nc, x_in, tok_in, ctx_in, ctxT_in, mask_in, gate0_in, w0_in, gate1_in, w1_in, out):
    B, S, D = x_in.shape
    T = B * S
    NT = T // P
    HW = T // 2
    TH = NT // 2
    NP = NT // 2
    C = D // P
    NEX, M = ctx_in.shape[:2]
    FC = M // P
    NA = NEX * FC
    U = [w0_in.shape[0], w1_in.shape[0]]
    E = [gate0_in.shape[2], gate1_in.shape[2]]
    SH = [U[0] - E[0], U[1] - E[1]]
    STEPS1 = 2 * TH + 4
    BK = [1, 3]
    GU = 4 * P
    WC = GU + D
    PER_EXPERT = VOCAB // NEX
    W = [w0_in, w1_in]
    assert HW == 512 and C == 2 and FC == 2 and S == 2 * P
    assert U[0] % 2 == 0 and U[1] % 2 == 1 and SH == [2, 1]

    cT_dram = [nc.dram_tensor(f"coef{l}_dram", (P, NT * 32), F32, kind="Internal").ap() for l in range(2)]

    with ExitStack() as stack:
        def sb(name, shape, dt=F32):
            return stack.enter_context(nc.sbuf_tensor(name, shape, dt))

        def sem(name):
            return stack.enter_context(nc.semaphore(name))

        ps = stack.enter_context(nc.psum_tensor("ps", [P, 8, HW], F32))

        def gate_bank(b):
            return ps[:, 2 * b, :]

        def up_bank(b):
            return ps[:, 2 * b + 1, :]

        def y_bank(c, h):
            return ps[:, 4 + 2 * c + h, :]

        def half(h):
            return slice(HW * h, HW * h + HW)

        x = sb("x", [P, NT, D])
        hn = sb("hn", [P, NT, D])
        hT = sb("hT", [P, C, T])
        hT_hi = sb("hT_hi", [P, C, T], F32R)
        hT_lo = sb("hT_lo", [P, C, T], F32R)
        yT = sb("yT", [P, C, T])
        stats = sb("stats", [P, NT, 6])
        meanvar = sb("meanvar", [P, NT, 2])
        veps = sb("veps", [P, NT])
        rstd = sb("rstd", [P, NT])
        shift = sb("shift", [P, NT])
        neghalf = sb("neghalf", [P, 2])
        warm = sb("warm", [P, 2])
        ident = sb("ident", [P, P])
        ctx_sb = sb("ctx_sb", [P, NEX, FC, D])
        ctxT_sb = sb("ctxT_sb", [P, NEX, C, M])
        ctxT_hi = sb("ctxT_hi", [P, NEX, C, M], F32R)
        ctxT_lo = sb("ctxT_lo", [P, NEX, C, M], F32R)
        tok = sb("tok", [P, T], I32)
        ge1 = sb("ge1", [P, T])
        ge2 = sb("ge2", [P, T])
        eid = sb("eid", [P, T])
        w_raw = sb("w_raw", [P, 2, WC])
        w_hi = sb("w_hi", [P, 2, WC], F32R)
        w_lo = sb("w_lo", [P, 2, WC], F32R)
        coef = sb("coef", [P, 2, 4, NT * 32])
        gated = sb("gated", [P, 2, HW])
        sil = sb("sil", [P, 2, HW])
        prod = sb("prod", [P, 2, HW])
        act = sb("act", [P, 2, HW])
        act_hi = sb("act_hi", [P, 2, 2, HW], F32R)
        act_lo = sb("act_lo", [P, 2, 2, HW], F32R)
        gate = [sb(f"gate{l}", [P, C, E[l]]) for l in range(2)]
        iota_i = sb("iota_i", [P, E[0]], I32)
        iota_f = sb("iota_f", [P, E[0]])
        scores = sb("scores", [P, NT, E[0]])
        gmax = sb("gmax", [P, NT, GROUPS])
        top_v = sb("top_v", [P, NT, 8])
        top_i = sb("top_i", [P, NT, 8], U32)
        top_f = sb("top_f", [P, NT, 8])
        g_eq = sb("g_eq", [P, NT, GROUPS, TOP_GROUPS])
        g_in = sb("g_in", [P, NT, GROUPS])
        s_in = sb("s_in", [P, NT, E[0]])
        s_cand = sb("s_cand", [P, NT, E[0]])
        w_sum = sb("w_sum", [P, NT])
        w_rec = sb("w_rec", [P, NT])
        at_least = sb("at_least", [P, NT, E[0]])
        tied = sb("tied", [P, NT, E[0]])
        behind = sb("behind", [P, NT, E[0]])
        ctok = [sb(f"ctok{l}", [P, NT, 32]) for l in range(2)]
        ctrn = [sb(f"ctrn{l}", [P, NT, 32]) for l in range(2)]
        probs = sb("probs", [P, NT, TOP_K1])
        e_eq = sb("e_eq", [P, NT, E[1], TOP_K1])
        e_w = sb("e_w", [P, NT, E[1], TOP_K1])
        mask_w = sb("mask_w", [P, B, M // 4], I32)
        mask_f = sb("mask_f", [P, B, M])
        mask_big = sb("mask_big", [P, B, M])
        valid = sb("valid", [P, B])
        negsc = sb("negsc", [P, NT, M])
        negmax = sb("negmax", [P, NT])
        esum = sb("esum", [P, NT])
        erec = sb("erec", [P, NT])
        escale = sb("escale", [P, NT])
        ex = yT[:, :, :].rearrange("p c n -> p (c n)").rearrange("p (t m) -> p t m", m=M)
        exT = sb("exT", [P, NT, FC, P])

        x_loaded = [sem(f"x_loaded{p}") for p in range(NP)]
        ctxT_loaded = [sem(f"ctxT_loaded{e}") for e in range(NEX)]
        ctx_loaded, tok_loaded = sem("ctx_loaded"), sem("tok_loaded")
        mask_loaded, gates_loaded = sem("mask_loaded"), sem("gates_loaded")
        ident_ready, iota_ready, mask_ready = sem("ident_ready"), sem("iota_ready"), sem("mask_ready")
        ident_zero, neghalf_ready, zeroed = sem("ident_zero"), sem("neghalf_ready"), sem("ctok_zeroed")
        ctx_hi_done, ctx_lo_done, ge_done = sem("ctx_hi_done"), sem("ctx_lo_done"), sem("ge_done")
        y_evac = [sem(f"y_evac{k}") for k in range(5)]
        y_turned = [sem(f"y_turned{k}") for k in range(5)]
        x_new = [sem(f"x_new{k}") for k in range(5)]
        st_done = [sem(f"st_done{k}") for k in range(4)]
        mv_done = [sem(f"mv_done{k}") for k in range(4)]
        ve_done = [sem(f"ve_done{k}") for k in range(4)]
        rs_done = [sem(f"rs_done{k}") for k in range(4)]
        sh_done = [sem(f"sh_done{k}") for k in range(4)]
        h_even = [sem(f"h_even{k}") for k in range(4)]
        h_odd = [sem(f"h_odd{k}") for k in range(4)]
        h_turned = [sem(f"h_turned{k}") for k in range(4)]
        hi_done = [sem(f"hT_hi_done{k}") for k in range(4)]
        lo_done = [sem(f"hT_lo_done{k}") for k in range(4)]
        hT_done = [sem(f"hT_done{k}") for k in range(4)]
        gu_done = [sem(f"gu_done{j}") for j in range(3)]
        gate_done = [sem(f"gate_done{j}") for j in range(3)]
        sil_done = [sem(f"sil_done{j}") for j in range(3)]
        prod_done = [sem(f"prod_done{j}") for j in range(3)]
        act_done = [sem(f"act_done{j}") for j in range(3)]
        act_hi_done = [sem(f"act_hi_done{j}") for j in range(3)]
        act_lo_done = [sem(f"act_lo_done{j}") for j in range(3)]
        down_done = [sem(f"down_done{j}") for j in range(3)]
        y_first = [sem(f"y_first{j}") for j in range(3)]
        gated_done = sem("gated_done")
        w_loaded = [[sem(f"w_loaded{l}_{s}") for s in range(2)] for l in range(2)]
        c_loaded = [[sem(f"c_loaded{l}_{s}") for s in range(2)] for l in range(2)]
        c_first = [sem(f"c_first{h}") for h in range(2)]
        wgu_hi = [sem(f"wgu_hi{l}") for l in range(2)]
        wgu_lo = [sem(f"wgu_lo{l}") for l in range(2)]
        wdn_hi = [sem(f"wdn_hi{l}") for l in range(2)]
        wdn_lo = [sem(f"wdn_lo{l}") for l in range(2)]
        logits_done = [sem(f"logits_done{l}") for l in range(2)]
        scores_done = [sem(f"scores_done{l}") for l in range(2)]
        route = [sem(f"route_step{l}") for l in range(2)]
        probs_done, iota_done = sem("probs_done"), sem("iota_f_done")
        ctrn_done = [sem(f"ctrn_done{l}") for l in range(2)]
        c_stored = [sem(f"c_stored{l}") for l in range(2)]
        s_done, sc_done = sem("s_done"), sem("sc_done")
        e_done, eT_done, eT_copied, pv_done = sem("e_done"), sem("eT_done"), sem("eT_copied"), sem("pv_done")
        rec_done, escale_done = sem("rec_done"), sem("escale_done")
        stored = sem("stored")

        x_v = x_in.rearrange("b s d -> (b s) d").rearrange("(t p) d -> p t d", p=P)
        out_v = out.rearrange("b s d -> (b s) d").rearrange("(t p) d -> p t d", p=P)

        UNIT_FIRST = [(0, 0), (0, 1), (1, 0), (1, 1)]
        HALF_FIRST = [(0, 0), (1, 0), (0, 1), (1, 1)]

        def last_groups(n_units):
            return [(2 * n_units - 4 + i, n_units - 2 + u, h) for i, (u, h) in enumerate(HALF_FIRST)]

        block = stack.enter_context(nc.Block())

        @block.sync
        def _(sp):
            def load_x(p):
                sp.dma_start(x[:, 2 * p:2 * p + 2, :], x_v[:, 2 * p:2 * p + 2, :]).then_inc(x_loaded[p], 16)

            def load_ctxT(e):
                sp.dma_start(ctxT_sb[:, e, :, :], ctxT_in[e].rearrange("(c p) m -> p c m", p=P))\
                  .then_inc(ctxT_loaded[e], 16)

            def load_w(l, n, s):
                sp.dma_start(w_raw[:, s, :], W[l][n, :, :]).then_inc(w_loaded[l][s], 16)

            def load_w_again(l, n, s):
                sp.wait_ge(wgu_lo[l], n - 1)
                sp.wait_ge(wdn_lo[l], n - 1)
                load_w(l, n, s)

            def load_c(l, n, s):
                sp.wait_ge(act_done[l + 1], 2 * n - 2)
                rows = cT_dram[l].rearrange("(q e) x -> e q x", q=4)
                sp.dma_start(coef[:, s, :, :], rows[n - SH[l], :, :].partition_broadcast(P))\
                  .then_inc(c_loaded[l][s], 16)

            def store_c(l, h=None):
                part = slice(0, NT * 32) if h is None else slice(TH * 32 * h, TH * 32 * h + TH * 32)
                count = 2 if h is None else h + 1
                sp.wait_ge(ctrn_done[l], count)
                sp.dma_start(cT_dram[l][:, part], ctrn[l][:, :, :].rearrange("p t j -> p (t j)")[:, part])\
                  .then_inc(c_stored[l], 16)
                sp.wait_ge(c_stored[l], 16 if h is None else 16 * h + 16)

            load_x(0)
            load_x(1)
            load_ctxT(0)
            load_x(2)
            load_x(3)
            sp.dma_start(tok[:, :], tok_in.partition_broadcast(P)).then_inc(tok_loaded, 16)
            for e in range(1, NEX):
                load_ctxT(e)
            load_w(0, 0, 0)
            load_w(0, 1, 1)
            sp.dma_start(gate[0][:, :, :], gate0_in).then_inc(gates_loaded, 16)
            sp.dma_start(gate[1][:, :, :], gate1_in).then_inc(gates_loaded, 16)
            sp.dma_start(ctx_sb[:, :, :, :], ctx_in.rearrange("b (c p) d -> p b c d", p=P)).then_inc(ctx_loaded, 16)
            sp.dma_start(mask_w[:, :, :], mask_in.partition_broadcast(P)).then_inc(mask_loaded, 16)
            load_w_again(0, 2, 0)
            load_w_again(0, 3, 1)
            store_c(0)
            load_c(0, 2, 0)
            load_c(0, 3, 1)
            with sp.Fori(2, U[0] // 2) as i:
                for s in range(2):
                    load_w_again(0, 2 * i + s, s)
                    load_c(0, 2 * i + s, s)
            sp.wait_ge(wgu_lo[0], U[0])
            sp.wait_ge(wdn_lo[0], U[0])
            load_w(1, 0, 0)
            load_w(1, 1, 1)
            load_w_again(1, 2, 0)
            load_w_again(1, 3, 1)
            sp.wait_ge(act_done[1], 2 * U[0])
            for h in range(2):
                store_c(1, h)
                part = slice(TH * 32 * h, TH * 32 * h + TH * 32)
                rows = cT_dram[1].rearrange("(q e) x -> e q x", q=4)
                sp.dma_start(coef[:, 1, :, part], rows[0, :, part].partition_broadcast(P)).then_inc(c_first[h], 16)
            load_c(1, 2, 0)
            load_c(1, 3, 1)
            with sp.Fori(2, U[1] // 2) as i:
                for s in range(2):
                    load_w_again(1, 2 * i + s, s)
                    load_c(1, 2 * i + s, s)
            load_w_again(1, U[1] - 1, 0)
            load_c(1, U[1] - 1, 0)
            for p in range(NP):
                sp.wait_ge(x_new[4], p + 1)
                sp.dma_start(out_v[:, 2 * p:2 * p + 2, :], x[:, 2 * p:2 * p + 2, :]).then_inc(stored, 16)
            sp.wait_ge(stored, 16 * NP)

        @block.gpsimd
        def _(pool):
            pool.memset(neghalf[:, :], -0.5).then_inc(neghalf_ready, 1)
            pool.memset(ident[:, :], 0.0).then_inc(ident_zero, 1)
            pool.wait_ge(ident_zero, 1)
            pool.affine_select(out=ident[:, :], in_=ident[:, :], compare_op=ALU.not_equal, fill=1.0,
                               base=0, pattern=[[-1, P]], channel_multiplier=1).then_inc(ident_ready, 1)
            pool.iota(iota_i[:, :], pattern=[[1, E[0]]], base=0, channel_multiplier=0).then_inc(iota_ready, 1)
            pool.wait_ge(neghalf_ready, 1)

            def inverse_std(k, p):
                r = slice(2 * p, 2 * p + 2)
                pool.wait_ge(mv_done[k], 2 * p + 2)
                pool.tensor_scalar(veps[:, r], meanvar[:, r, 1], EPS, None, ALU.add).then_inc(ve_done[k], 1)
                pool.wait_ge(ve_done[k], p + 1)
                pool.tensor_tensor(rstd[:, r], veps[:, r], neghalf[:, :], ALU.pow).then_inc(rs_done[k], 1)
                pool.wait_ge(rs_done[k], p + 1)
                t = 2 * p + 1
                pool.tensor_scalar(shift[:, t:t + 1], meanvar[:, t, 0:1], rstd[:, t:t + 1], -1.0,
                                   ALU.mult, ALU.mult).then_inc(sh_done[k], 1)

            def split_act(j, g, b, s, h, read):
                pool.wait_ge(act_hi_done[j], g + 1)
                if read is not None:
                    pool.wait_ge(down_done[j], read)
                pool.tensor_tensor(act_lo[:, s, h, :], act[:, b, :], act_hi[:, s, h, :].bitcast(F32),
                                   ALU.subtract).then_inc(act_lo_done[j], 1)

            def split_a(g):
                split_act(0, g, g % 2, g // 2 % 2, g % 2, g - 3 if g >= 4 else None)

            for p in range(NP):
                inverse_std(0, p)
            for g in range(NA + 5):
                split_a(g)
            inverse_std(1, 0)
            inverse_std(1, 1)
            for g in range(NA + 5, 2 * NA):
                split_a(g)
            split_act(1, 0, 0, 0, 0, None)
            inverse_std(1, 2)
            inverse_std(1, 3)
            split_act(1, 1, 1, 1, 0, None)
            split_act(1, 2, 0, 0, 1, None)
            split_act(1, 3, 1, 1, 1, None)
            for l in range(2):
                j = l + 1
                if l == 1:
                    for g, (n, h) in enumerate(UNIT_FIRST):
                        split_act(j, g, h, n, h, None)
                with pool.Fori(1, (U[l] - 2) // 2) as q:
                    for s in range(2):
                        for h in range(2):
                            split_act(j, 4 * q + 2 * s + h, h, s, h, 4 * q + 2 * s + h - 3)
                if l == 1:
                    split_act(j, 2 * U[l] - 6, 0, 0, 0, 2 * U[l] - 9)
                    split_act(j, 2 * U[l] - 5, 1, 0, 1, 2 * U[l] - 8)
                for g, n, h in last_groups(U[l]):
                    split_act(j, g, g % 2, n % 2, h, 2 * n + h - 3)
                if l == 0:
                    for k in (2, 3):
                        for p in range(NP):
                            inverse_std(k, p)

        @block.scalar
        def _(a):
            def round_gate_up(l, q, s, reuse=True):
                a.wait_ge(w_loaded[l][s], 16 * q + 16)
                if reuse:
                    a.wait_ge(gu_done[l + 1], 4 * q + 2 * s - 2)
                a.activation(w_hi[:, s, 0:GU], w_raw[:, s, 0:GU], ACT.Copy).then_inc(wgu_hi[l], 1)

            def round_down(l, q, s, reuse=True):
                if reuse:
                    a.wait_ge(down_done[l + 1], 4 * q + 2 * s - 2)
                a.activation(w_hi[:, s, GU:WC], w_raw[:, s, GU:WC], ACT.Copy).then_inc(wdn_hi[l], 1)

            def evac_y(k, j, downs, h):
                for c in range(C):
                    if c == 0:
                        a.wait_ge(y_first[j], h + 1)
                    else:
                        a.wait_ge(down_done[j], downs)
                    a.activation(yT[:, c, half(h)], y_bank(c, h), ACT.Copy).then_inc(y_evac[k], 1)

            def norm_odd(k, p):
                t = 2 * p + 1
                a.wait_ge(sh_done[k], p + 1)
                a.activation(hn[:, t, :], x[:, t, :], ACT.Identity, bias=shift[:, t:t + 1],
                             scale=rstd[:, t:t + 1]).then_inc(h_odd[k], 1)

            def turned_hi(k, h):
                a.wait_ge(h_turned[k], h + 1)
                for c in range(C):
                    a.activation(hT_hi[:, c, half(h)], y_bank(c, h), ACT.Copy).then_inc(hi_done[k], 1)

            def turned_whole(k, h):
                a.wait_ge(h_turned[k], h + 1)
                for c in range(C):
                    a.activation(hT[:, c, half(h)], y_bank(c, h), ACT.Copy).then_inc(hT_done[k], 1)

            def turned_both(k, h):
                turned_whole(k, h)
                rounded(k, h)

            def rounded(k, h):
                for c in range(C):
                    a.wait_ge(hT_done[k], 2 * h + c + 1)
                    a.activation(hT_hi[:, c, half(h)], hT[:, c, half(h)], ACT.Copy).then_inc(hi_done[k], 1)

            def silu(j, g, b, src, fresh=False):
                if not fresh:
                    a.wait_ge(act_done[j], g - 1)
                a.activation(sil[:, b, :], src, ACT.Silu).then_inc(sil_done[j], 1)

            def silu_gate(j, g, b, fresh=False):
                a.wait_ge(gate_done[j], g + 1)
                silu(j, g, b, gate_bank(b), fresh)

            def silu_gated(g, b):
                a.wait_ge(gated_done, g - 2 * SH[1] + 1)
                silu(2, g, b, gated[:, b, :])

            def round_act(j, g, b, n, s, h, reuse=True):
                a.wait_ge(act_done[j], g + 1)
                if reuse:
                    a.wait_ge(down_done[j], 2 * n + h - 3)
                a.activation(act_hi[:, s, h, :], act[:, b, :], ACT.Copy).then_inc(act_hi_done[j], 1)

            def step(l, q, s):
                n = 2 * q + s
                round_gate_up(l, q + s, 1 - s)
                round_down(l, q, s)
                for h in range(2):
                    if l == 1:
                        silu_gated(2 * n + h, h)
                    else:
                        silu_gate(1, 2 * n + h, h)
                for h in range(2):
                    round_act(l + 1, 2 * n + h, h, n, s, h)

            def tail(l):
                j, k, N = l + 1, BK[l] + 1, U[l]
                groups = last_groups(N)

                def silu_last(i):
                    g = groups[i][0]
                    if l == 1:
                        silu_gated(g, g % 2)
                    else:
                        silu_gate(j, g, g % 2)

                def round_last(i):
                    g, n, h = groups[i]
                    round_act(j, g, g % 2, n, n % 2, h)

                round_gate_up(l, (N - 1) // 2, (N - 1) % 2)
                round_down(l, (N - 2) // 2, N % 2)
                silu_last(0)
                silu_last(1)
                round_last(0)
                round_last(1)
                round_down(l, (N - 1) // 2, (N - 1) % 2)
                silu_last(2)
                round_last(2)
                if k < 4:
                    evac_y(k, j, 2 * N - 2, 0)
                    silu_last(3)
                    round_last(3)
                    norm_odd(k, 0)
                    norm_odd(k, 1)
                    evac_y(k, j, 2 * N, 1)
                    turned_whole(k, 0)
                else:
                    silu_last(3)
                    round_last(3)
                    evac_y(k, j, 2 * N - 2, 0)
                    evac_y(k, j, 2 * N, 1)

            def round_ctxT(e):
                a.wait_ge(ctxT_loaded[e], 16)
                a.activation(ctxT_hi[:, e, :, :], ctxT_sb[:, e, :, :], ACT.Copy).then_inc(ctx_hi_done, 1)

            a.wait_ge(neghalf_ready, 1)
            a.activation(warm[:, :], neghalf[:, :], ACT.Silu)
            norm_odd(0, 0)
            round_ctxT(0)
            norm_odd(0, 1)
            turned_hi(0, 0)
            norm_odd(0, 2)
            round_ctxT(1)
            norm_odd(0, 3)
            def silu_a(g):
                a.wait_ge(gu_done[0], g + 1)
                silu(0, g, g % 2, ps[:, g % 4, :], fresh=(g < 2))

            def round_a(g):
                a.wait_ge(act_done[0], g + 1)
                if g >= 4:
                    a.wait_ge(down_done[0], g - 3)
                a.activation(act_hi[:, g // 2 % 2, g % 2, :], act[:, g % 2, :], ACT.Copy).then_inc(act_hi_done[0], 1)

            def sigmoid_scores(h):
                a.wait_ge(logits_done[0], h + 1)
                a.activation(scores[:, TH * h:TH * h + TH, :],
                             y_bank(1, h)[:, 0:TH * E[0]].rearrange("p (t e) -> p t e", e=E[0]),
                             ACT.Sigmoid).then_inc(scores_done[0], 1)

            for g in range(NA + 4):
                silu_a(g)
                if g in (0, 2):
                    round_ctxT(g // 2 + 2)
                if g >= 1:
                    round_a(g - 1)
                if g == 0:
                    turned_hi(0, 1)
                if g == 6:
                    round_gate_up(0, 0, 0, False)
                    round_down(0, 0, 0, False)
                if g == 8:
                    round_gate_up(0, 0, 1, False)
                    round_down(0, 0, 1, False)
            round_a(NA + 3)
            evac_y(1, 0, NA, 0)
            silu_a(NA + 4)
            round_a(NA + 4)
            silu_a(NA + 5)
            round_a(NA + 5)
            silu_a(NA + 6)
            norm_odd(1, 0)
            norm_odd(1, 1)
            turned_whole(1, 0)
            silu_a(NA + 7)
            round_a(NA + 6)
            rounded(1, 0)
            round_a(NA + 7)
            sigmoid_scores(0)
            evac_y(1, 0, 2 * NA, 1)
            silu_gate(1, 0, 0, fresh=True)
            round_act(1, 0, 0, 0, 0, 0, False)
            silu_gate(1, 1, 1, fresh=True)
            norm_odd(1, 2)
            round_act(1, 1, 1, 1, 1, 0, False)
            norm_odd(1, 3)
            turned_both(1, 1)
            sigmoid_scores(1)
            silu_gate(1, 2, 0)
            a.wait_ge(gu_done[1], 3)
            round_gate_up(0, 1, 0, False)
            round_act(1, 2, 0, 0, 0, 1, False)
            silu_gate(1, 3, 1)
            round_act(1, 3, 1, 1, 1, 1, False)
            a.wait_ge(down_done[1], 3)
            with a.Fori(1, U[0] // 2 - 1) as q:
                for s in range(2):
                    step(0, q, s)
            tail(0)
            for i in range(NT + 2):
                if i < NT:
                    a.wait_ge(sc_done, i + 1)
                    a.activation(ex[:, i, :], negsc[:, i, :], ACT.Exp, bias=negmax[:, i:i + 1], scale=-1.0,
                                 accum_out=esum[:, i:i + 1]).then_inc(e_done, 1)
                if i == 0:
                    norm_odd(2, 2)
                    norm_odd(2, 3)
                if i >= 1 and i - 1 < NT:
                    t = i - 1
                    a.wait_ge(eT_done, t + 1)
                    a.activation(exT[:, t, :, :], ps[:, 2 + t % 2, 0:M].rearrange("p (c q) -> p c q", c=FC),
                                 ACT.Copy).then_inc(eT_copied, 1)
                if i == 1:
                    turned_whole(2, 1)
                if i == 3:
                    round_gate_up(1, 0, 0, False)
                    round_down(1, 0, 0, False)
                    round_gate_up(1, 0, 1, False)
                    round_down(1, 0, 1, False)
                if i in (5, 7, 9):
                    norm_odd(3, (i - 5) // 2)
                if i == 8:
                    turned_both(3, 0)
            def copy_scores(h):
                a.wait_ge(logits_done[1], h + 1)
                a.activation(scores[:, TH * h:TH * h + TH, 0:E[1]],
                             y_bank(1, h)[:, 0:TH * E[1]].rearrange("p (t e) -> p t e", e=E[1]),
                             ACT.Copy).then_inc(scores_done[1], 1)

            def top_probs(h):
                a.wait_ge(route[1], STEPS1 * h + TH)
                a.activation(probs[:, TH * h:TH * h + TH, :], top_v[:, TH * h:TH * h + TH, 0:TOP_K1],
                             ACT.Sigmoid).then_inc(probs_done, 1)

            copy_scores(0)
            top_probs(0)
            norm_odd(3, 3)
            turned_both(3, 1)
            copy_scores(1)
            silu_gate(2, 0, 0, fresh=True)
            silu_gate(2, 1, 1, fresh=True)
            round_act(2, 0, 0, 0, 0, 0, False)
            top_probs(1)
            round_act(2, 1, 1, 0, 0, 1, False)
            round_gate_up(1, 1, 0)
            silu_gated(2, 0)
            round_act(2, 2, 0, 1, 1, 0, False)
            silu_gated(3, 1)
            round_act(2, 3, 1, 1, 1, 1, False)
            with a.Fori(1, (U[1] - 2) // 2) as q:
                for s in range(2):
                    step(1, q, s)
            step(1, (U[1] - 3) // 2, 0)
            tail(1)

        @block.vector
        def _(v):
            v.memset(ctok[1][:, :, :], 0.0).then_inc(zeroed, 1)

            def add_pair(k, p):
                v.wait_ge(y_turned[k], p + 1)
                v.tensor_tensor(x[:, 2 * p:2 * p + 2, :], x[:, 2 * p:2 * p + 2, :],
                                y_bank(p % 2, p // 2).rearrange("p (t d) -> p t d", d=D),
                                ALU.add).then_inc(x_new[k], 1)

            def moments(k, p):
                for t in (2 * p, 2 * p + 1):
                    if k == 0:
                        v.wait_ge(x_loaded[p], 16)
                    else:
                        v.wait_ge(x_new[k], t + 1 if k == 3 else p + 1)
                    v.bn_stats(stats[:, t, :], x[:, t, :]).then_inc(st_done[k], 1)
                for t in (2 * p, 2 * p + 1):
                    v.wait_ge(st_done[k], t + 1)
                    v.bn_aggr(meanvar[:, t, :], stats[:, t, :]).then_inc(mv_done[k], 1)

            def norm_even(k, p):
                t = 2 * p
                v.wait_ge(rs_done[k], p + 1)
                v.tensor_scalar(hn[:, t, :], x[:, t, :], meanvar[:, t, 0:1], rstd[:, t:t + 1],
                                ALU.subtract, ALU.mult).then_inc(h_even[k], 1)

            def turned_lo(k, h):
                for c in range(C):
                    v.wait_ge(hi_done[k], 2 * h + c + 1)
                    v.tensor_tensor(hT_lo[:, c, half(h)], y_bank(c, h) if k == 0 else hT[:, c, half(h)],
                                    hT_hi[:, c, half(h)].bitcast(F32),
                                    ALU.subtract).then_inc(lo_done[k], 1)

            def rest_gate_up(l, n, s):
                v.wait_ge(wgu_hi[l], n + 1)
                v.tensor_tensor(w_lo[:, s, 0:GU], w_raw[:, s, 0:GU], w_hi[:, s, 0:GU].bitcast(F32),
                                ALU.subtract).then_inc(wgu_lo[l], 1)

            def rest_down(l, n, s):
                v.wait_ge(wdn_hi[l], n + 1)
                v.tensor_tensor(w_lo[:, s, GU:WC], w_raw[:, s, GU:WC], w_hi[:, s, GU:WC].bitcast(F32),
                                ALU.subtract).then_inc(wdn_lo[l], 1)

            def plain(j, g, b, fresh=False):
                v.wait_ge(sil_done[j], g + 1)
                v.wait_ge(gu_done[j], g + 1)
                if not fresh:
                    v.wait_ge(act_lo_done[j], g - 1)
                v.tensor_tensor(act[:, b, :], sil[:, b, :], up_bank(b), ALU.mult).then_inc(act_done[j], 1)

            def by_block(a):
                return a.rearrange("p (t q j) -> p t q j", q=4, j=32)

            def half_coef(s, h):
                return coef[:, s, :, :].rearrange("p q (t j) -> p t q j", j=32)[:, TH * h:TH * h + TH, :, :]

            def times_prob(g, b, s, h):
                v.wait_ge(gate_done[2], g + 1)
                v.tensor_tensor(by_block(gated[:, b, :]), by_block(gate_bank(b)), half_coef(s, h),
                                ALU.mult).then_inc(gated_done, 1)

            def times_up(j, g, b, up):
                v.wait_ge(sil_done[j], g + 1)
                if j > 0:
                    v.wait_ge(gu_done[j], g + 1)
                v.tensor_tensor(prod[:, b, :], sil[:, b, :], up, ALU.mult).then_inc(prod_done[j], 1)

            def times_coef(l, g, b, s, h):
                v.wait_ge(prod_done[l + 1], g - 2 * SH[l] + 1)
                v.wait_ge(act_lo_done[l + 1], g - 1)
                v.tensor_tensor(by_block(act[:, b, :]), by_block(prod[:, b, :]), half_coef(s, h), ALU.mult)\
                 .then_inc(act_done[l + 1], 1)

            def routed(l, groups):
                if l == 1:
                    for i, (g, q, s, h) in enumerate(groups):
                        v.wait_ge(c_loaded[1][s], 16 * q)
                        times_prob(g, i, s, h)
                for i, (g, q, s, h) in enumerate(groups):
                    times_up(l + 1, g, i, up_bank(i))
                for i, (g, q, s, h) in enumerate(groups):
                    if l == 0:
                        v.wait_ge(c_loaded[0][s], 16 * q)
                    times_coef(l, g, i, s, h)

            def last_routed(l, i):
                g, n, h = last_groups(U[l])[i]
                q, s, b = n // 2, n % 2, g % 2
                if l == 1:
                    times_prob(g, b, s, h)
                times_up(l + 1, g, b, up_bank(b))
                times_coef(l, g, b, s, h)

            def step(l, q, s):
                n = 2 * q + s
                rest_gate_up(l, n + 1, 1 - s)
                rest_down(l, n, s)
                routed(l, [(2 * n + h, q, s, h) for h in range(2)])

            def tail(l):
                k, N = BK[l] + 1, U[l]
                rest_gate_up(l, N - 1, (N - 1) % 2)
                rest_down(l, N - 2, N % 2)
                routed(l, [(g, n // 2, n % 2, h) for g, n, h in last_groups(N)[0:2]])
                rest_down(l, N - 1, (N - 1) % 2)
                last_routed(l, 2)
                if k < 4:
                    add_pair(k, 0)
                    moments(k, 0)
                    last_routed(l, 3)
                    add_pair(k, 1)
                    moments(k, 1)
                    norm_even(k, 0)
                    norm_even(k, 1)
                else:
                    last_routed(l, 3)
                    add_pair(k, 0)
                    add_pair(k, 1)

            def rest_ctxT(e):
                v.wait_ge(ctx_hi_done, e + 1)
                v.tensor_tensor(ctxT_lo[:, e, :, :], ctxT_sb[:, e, :, :], ctxT_hi[:, e, :, :].bitcast(F32),
                                ALU.subtract).then_inc(ctx_lo_done, 1)

            moments(0, 0)
            moments(0, 1)
            norm_even(0, 0)
            norm_even(0, 1)
            rest_ctxT(0)
            moments(0, 2)
            turned_lo(0, 0)
            moments(0, 3)
            norm_even(0, 2)
            rest_ctxT(1)
            norm_even(0, 3)
            v.wait_ge(tok_loaded, 16)

            def token_experts(h):
                v.tensor_scalar(ge1[:, half(h)], tok[:, half(h)], float(PER_EXPERT), None, ALU.is_ge)\
                 .then_inc(ge_done, 1)
                v.wait_ge(ge_done, 3 * h + 1)
                v.scalar_tensor_tensor(ge2[:, half(h)], tok[:, half(h)], float(2 * PER_EXPERT), ge1[:, half(h)],
                                       ALU.is_ge, ALU.add).then_inc(ge_done, 1)
                v.wait_ge(ge_done, 3 * h + 2)
                v.scalar_tensor_tensor(eid[:, half(h)], tok[:, half(h)], float(3 * PER_EXPERT), ge2[:, half(h)],
                                       ALU.is_ge, ALU.add).then_inc(ge_done, 1)

            token_experts(0)
            def masked(g):
                b, n, h = g % 2, g % NA, g // NA
                if n == 0:
                    v.wait_ge(ge_done, 3 * h + 3)
                times_up(0, g, b, ps[:, g % 4, :])
                v.wait_ge(prod_done[0], g + 1)
                if g >= 2:
                    v.wait_ge(act_lo_done[0], g - 1)
                v.scalar_tensor_tensor(act[:, b, :], eid[:, half(h)], float(n // FC), prod[:, b, :],
                                       ALU.is_equal, ALU.mult).then_inc(act_done[0], 1)

            STEPS = 8 + 4 * TH + 9
            K = TOP_K0 - 1
            three = [P, TH, E[0]]

            def route_groups(h):
                r, at = slice(TH * h, TH * h + TH), STEPS * h
                v.wait_ge(scores_done[0], h + 1)
                v.tensor_reduce(gmax[:, r, :], scores[:, r, :].rearrange("p t (g j) -> p t g j", g=GROUPS), AX_X,
                                ALU.max).then_inc(route[0], 1)
                v.wait_ge(route[0], at + 1)
                for t in range(TH):
                    v.max(top_v[:, TH * h + t, :], gmax[:, TH * h + t, :]).then_inc(route[0], 1)
                for t in range(TH):
                    v.wait_ge(route[0], at + 2 + t)
                    v.max_index(top_i[:, TH * h + t, :], top_v[:, TH * h + t, :],
                                gmax[:, TH * h + t, :]).then_inc(route[0], 1)
                at += 1 + 2 * TH
                v.wait_ge(route[0], at)
                v.tensor_copy(top_f[:, r, :], top_i[:, r, :]).then_inc(route[0], 1)
                v.wait_ge(route[0], at + 1)
                four = [P, TH, GROUPS, TOP_GROUPS]
                v.tensor_tensor(g_eq[:, r, :, :],
                                iota_f[:, 0:GROUPS].unsqueeze(1).unsqueeze(3).to_broadcast(four),
                                top_f[:, r, 0:TOP_GROUPS].unsqueeze(2).to_broadcast(four),
                                ALU.is_equal).then_inc(route[0], 1)
                v.wait_ge(route[0], at + 2)
                v.tensor_reduce(g_in[:, r, :], g_eq[:, r, :, :], AX_X, ALU.add).then_inc(route[0], 1)
                v.wait_ge(route[0], at + 3)
                four = [P, TH, GROUPS, E[0] // GROUPS]
                sc_v, si_v, ca_v = (a[:, r, :].rearrange("p t (g j) -> p t g j", g=GROUPS)
                                    for a in (scores, s_in, s_cand))
                v.tensor_tensor(si_v, sc_v, g_in[:, r, :].unsqueeze(3).to_broadcast(four),
                                ALU.mult).then_inc(route[0], 1)
                v.tensor_scalar(gmax[:, r, :], g_in[:, r, :], -1.0, None, ALU.add).then_inc(route[0], 1)
                v.wait_ge(route[0], at + 5)
                v.tensor_tensor(ca_v, si_v, gmax[:, r, :].unsqueeze(3).to_broadcast(four),
                                ALU.add).then_inc(route[0], 1)

            def route_experts(h):
                r, at = slice(TH * h, TH * h + TH), STEPS * h + 2 * TH + 7
                v.wait_ge(route[0], at)
                for t in range(TH):
                    v.max(top_v[:, TH * h + t, :], s_cand[:, TH * h + t, :]).then_inc(route[0], 1)
                for t in range(TH):
                    v.wait_ge(route[0], at + 1 + t)
                    v.max_index(top_i[:, TH * h + t, :], top_v[:, TH * h + t, :],
                                s_cand[:, TH * h + t, :]).then_inc(route[0], 1)
                v.tensor_reduce(w_sum[:, r], top_v[:, r, 0:TOP_K0], AX_X, ALU.add).then_inc(route[0], 1)
                v.tensor_tensor(at_least[:, r, :], s_cand[:, r, :], top_v[:, r, K:K + 1].to_broadcast(three),
                                ALU.is_ge).then_inc(route[0], 1)
                v.tensor_tensor(tied[:, r, :], s_cand[:, r, :], top_v[:, r, K:K + 1].to_broadcast(three),
                                ALU.is_equal).then_inc(route[0], 1)

            def route_weights(h):
                r, at = slice(TH * h, TH * h + TH), STEPS * h + 4 * TH + 7
                v.wait_ge(route[0], at + 1)
                v.reciprocal(w_rec[:, r], w_sum[:, r]).then_inc(route[0], 1)
                v.tensor_copy(top_f[:, r, :], top_i[:, r, :]).then_inc(route[0], 1)
                v.wait_ge(route[0], at + 5)
                v.tensor_tensor(behind[:, r, :], iota_f[:, :].unsqueeze(1).to_broadcast(three),
                                top_f[:, r, K:K + 1].to_broadcast(three), ALU.is_gt).then_inc(route[0], 1)
                v.scalar_tensor_tensor(s_in[:, r, :], scores[:, r, :], ROUTE_SCALE,
                                       w_rec[:, r].unsqueeze(2).to_broadcast(three), ALU.mult, ALU.mult)\
                 .then_inc(route[0], 1)
                v.wait_ge(route[0], at + 7)
                v.tensor_tensor(tied[:, r, :], tied[:, r, :], behind[:, r, :], ALU.mult).then_inc(route[0], 1)
                v.wait_ge(route[0], at + 8)
                v.tensor_tensor(at_least[:, r, :], at_least[:, r, :], tied[:, r, :],
                                ALU.subtract).then_inc(route[0], 1)
                v.wait_ge(route[0], at + 9)
                v.tensor_tensor(ctok[0][:, r, :], at_least[:, r, :], s_in[:, r, :], ALU.mult).then_inc(route[0], 1)
                v.wait_ge(route[0], at + 10)
                v.transpose(ctrn[0][:, r, :].rearrange("p t e -> p (t e)"),
                            ctok[0][:, r, :].rearrange("p t e -> p (t e)")).then_inc(ctrn_done[0], 1)

            v.wait_ge(iota_ready, 1)
            v.tensor_copy(iota_f[:, :], iota_i[:, :]).then_inc(iota_done, 1)
            for g in range(NA + 5):
                masked(g)
                if g in (0, 2):
                    rest_ctxT(g // 2 + 2)
                if g == 1:
                    turned_lo(0, 1)
                if g == 3:
                    token_experts(1)
                if g == 7:
                    rest_gate_up(0, 0, 0)
                    rest_down(0, 0, 0)
                if g == 9:
                    rest_gate_up(0, 1, 1)
                    rest_down(0, 1, 1)
            add_pair(1, 0)
            moments(1, 0)
            add_pair(1, 1)
            moments(1, 1)
            masked(NA + 5)
            norm_even(1, 0)
            norm_even(1, 1)
            masked(NA + 6)
            masked(NA + 7)
            turned_lo(1, 0)
            v.wait_ge(iota_done, 1)
            route_groups(0)
            add_pair(1, 2)
            plain(1, 0, 0, fresh=True)
            moments(1, 2)
            add_pair(1, 3)
            moments(1, 3)
            plain(1, 1, 1, fresh=True)
            norm_even(1, 2)
            norm_even(1, 3)
            route_experts(0)
            turned_lo(1, 1)
            route_weights(0)
            route_groups(1)
            plain(1, 2, 0)
            rest_gate_up(0, 2, 0)
            route_experts(1)
            plain(1, 3, 1)
            route_weights(1)
            v.wait_ge(mask_loaded, 16)
            v.tensor_copy(mask_f[:, :, :], mask_w[:, :, :].bitcast(U8)).then_inc(mask_ready, 1)
            v.wait_ge(mask_ready, 1)
            v.tensor_scalar(mask_big[:, :, :], mask_f[:, :, :], -1.0, MASKED, ALU.add, ALU.mult)\
             .then_inc(mask_ready, 1)
            v.tensor_reduce(valid[:, :], mask_f[:, :, :], AX_X, ALU.max).then_inc(mask_ready, 1)
            v.wait_ge(mask_ready, 3)

            with v.Fori(1, U[0] // 2 - 1) as q:
                for s in range(2):
                    step(0, q, s)
            tail(0)
            add_pair(2, 2)
            moments(2, 2)
            for i in range(NT + 4):
                if i < NT:
                    b = i // 2
                    v.wait_ge(s_done, i + 1)
                    v.tensor_tensor_reduce(out=negsc[:, i, :], in0=ps[:, i % 2, 0:M], in1=mask_big[:, b, :],
                                           scale=-float(D) ** -0.5, scalar=3e38, op0=ALU.add, op1=ALU.min,
                                           accum_out=negmax[:, i:i + 1]).then_inc(sc_done, 1)
                if i == 0:
                    add_pair(2, 3)
                    moments(2, 3)
                    norm_even(2, 2)
                if i == 1:
                    norm_even(2, 3)
                if i == 4:
                    rest_gate_up(1, 0, 0)
                    rest_down(1, 0, 0)
                    rest_gate_up(1, 1, 1)
                    rest_down(1, 1, 1)
                if i >= 3 and i - 3 < NT:
                    t = i - 3
                    p = t // 2
                    if t % 2 == 0:
                        v.wait_ge(e_done, t + 2)
                        v.reciprocal(erec[:, t:t + 2], esum[:, t:t + 2]).then_inc(rec_done, 1)
                        v.wait_ge(rec_done, p + 1)
                        v.tensor_scalar(escale[:, t:t + 2], erec[:, t:t + 2], valid[:, p:p + 1], None,
                                        ALU.mult).then_inc(escale_done, 1)
                        v.wait_ge(escale_done, p + 1)
                    v.wait_ge(pv_done, t + 1)
                    v.scalar_tensor_tensor(x[:, t, :], y_bank(t % 2, t // TH)[:, 0:D], escale[:, t:t + 1], x[:, t, :],
                                           ALU.mult, ALU.add).then_inc(x_new[3], 1)
                    if t % 2 == 1:
                        moments(3, p)
                if i in (5, 7, 9):
                    norm_even(3, (i - 5) // 2)
                if i == 9:
                    turned_lo(3, 0)
            def route_top(h):
                v.wait_ge(scores_done[1], h + 1)
                for t in range(TH * h, TH * h + TH):
                    v.max(top_v[:, t, :], scores[:, t, 0:E[1]]).then_inc(route[1], 1)
                for t in range(TH * h, TH * h + TH):
                    v.wait_ge(route[1], STEPS1 * h + t - TH * h + 1)
                    v.max_index(top_i[:, t, :], top_v[:, t, :], scores[:, t, 0:E[1]]).then_inc(route[1], 1)

            def route_top_weights(h):
                r, at = slice(TH * h, TH * h + TH), STEPS1 * h + 2 * TH
                four = [P, TH, E[1], TOP_K1]
                v.wait_ge(route[1], at)
                v.tensor_copy(top_f[:, r, :], top_i[:, r, :]).then_inc(route[1], 1)
                v.wait_ge(route[1], at + 1)
                v.tensor_tensor(e_eq[:, r, :, :], iota_f[:, 0:E[1]].unsqueeze(1).unsqueeze(3).to_broadcast(four),
                                top_f[:, r, 0:TOP_K1].unsqueeze(2).to_broadcast(four),
                                ALU.is_equal).then_inc(route[1], 1)
                if h == 1:
                    plain(2, 1, 1, fresh=True)
                v.wait_ge(route[1], at + 2)
                v.wait_ge(probs_done, h + 1)
                v.tensor_tensor(e_w[:, r, :, :], e_eq[:, r, :, :],
                                probs[:, r, :].unsqueeze(2).to_broadcast(four), ALU.mult).then_inc(route[1], 1)
                v.wait_ge(route[1], at + 3)
                v.wait_ge(zeroed, 1)
                v.tensor_reduce(ctok[1][:, r, 0:E[1]], e_w[:, r, :, :], AX_X, ALU.add).then_inc(route[1], 1)
                v.wait_ge(route[1], at + 4)
                v.transpose(ctrn[1][:, r, :].rearrange("p t e -> p (t e)"),
                            ctok[1][:, r, :].rearrange("p t e -> p (t e)")).then_inc(ctrn_done[1], 1)

            route_top(0)
            norm_even(3, 3)
            route_top_weights(0)
            turned_lo(3, 1)
            route_top(1)
            plain(2, 0, 0, fresh=True)
            route_top_weights(1)
            rest_gate_up(1, 2, 0)
            for h in range(2):
                v.wait_ge(c_first[h], 16)
                times_prob(2 + h, h, 1, h)
                times_up(2, 2 + h, h, up_bank(h))
                times_coef(1, 2 + h, h, 1, h)
            with v.Fori(1, (U[1] - 2) // 2) as q:
                for s in range(2):
                    step(1, q, s)
            step(1, (U[1] - 3) // 2, 0)
            tail(1)
            add_pair(4, 2)
            add_pair(4, 3)

        @block.tensor
        def _(pe):
            def split_product(dst, w_h, w_l, m_h, m_l, start, stop):
                pe.matmul(dst, w_h, m_h, start=start, stop=False)
                pe.matmul(dst, w_h, m_l, start=False, stop=False)
                return pe.matmul(dst, w_l, m_h, start=False, stop=stop)

            def keep_clock(n):
                for _ in range(n):
                    pe.matmul(gate_bank(0)[:, 0:P], ident[:, :], ident[:, :], start=True, stop=True)

            def turn_sums(k, h):
                pe.wait_ge(y_evac[k], 2 * h + 2)
                for t in range(TH * h, TH * h + TH):
                    p = t // 2
                    for c in range(C):
                        at = D * (t % 2) + P * c
                        mm = pe.transpose(y_bank(p % 2, h)[:, at:at + P], yT[:, c, P * t:P * t + P], ident[:, :])
                    if t % 2 == 1:
                        mm.then_inc(y_turned[k], 1)

            def turn_norm(k, h):
                if k in (1, 2):
                    pe.wait_ge(x_new[k], 2 * h + 2)
                elif k == 3:
                    pe.wait_ge(x_new[3], TH * h + TH)
                for t in range(TH * h, TH * h + TH):
                    if t % 2 == 0:
                        pe.wait_ge(h_even[k], t // 2 + 1)
                    else:
                        pe.wait_ge(h_odd[k], t // 2 + 1)
                    for c in range(C):
                        mm = pe.transpose(y_bank(c, h)[:, P * (t % TH):P * (t % TH) + P],
                                          hn[:, t, P * c:P * c + P], ident[:, :])
                mm.then_inc(h_turned[k], 1)

            def gate_up(l, g, b, s, h, before="routed", between=None):
                if before == "routed":
                    pe.wait_ge(prod_done[l + 1], g - 1 - 2 * SH[l])
                elif before == "shared":
                    pe.wait_ge(act_done[l + 1], g - 1)
                for o, dst in ((0, gate_bank(b)), (2 * P, up_bank(b))):
                    if o and between:
                        between()
                    for c in range(C):
                        w = slice(o + P * c, o + P * c + P)
                        mm = split_product(dst, w_hi[:, s, w], w_lo[:, s, w], hT_hi[:, c, half(h)],
                                           hT_lo[:, c, half(h)], c == 0, c == C - 1)
                    if o == 0:
                        mm.then_inc(gate_done[l + 1], 1)
                mm.then_inc(gu_done[l + 1], 1)

            def unit_up(l, n, s, before="routed"):
                pe.wait_ge(wgu_lo[l], n + 1)
                for h in range(2):
                    gate_up(l, 2 * n + h, h, s, h, before)

            def down(j, g, s, h, w_h, w_l, first=False, last=False, place=None):
                place = h if place is None else place
                pe.wait_ge(act_lo_done[j], g + 1)
                for c in range(C):
                    w = slice(P * c, P * c + P)
                    mm = split_product(y_bank(c, h), w_h[:, w], w_l[:, w], act_hi[:, s, place, :],
                                       act_lo[:, s, place, :], first, last)
                    if last and c == 0:
                        mm.then_inc(y_first[j], 1)
                mm.then_inc(down_done[j], 1)

            def unit_down(l, n, s, first=False):
                pe.wait_ge(wdn_lo[l], n + 1)
                for h in range(2):
                    down(l + 1, 2 * n + h, s, h, w_hi[:, s, GU:WC], w_lo[:, s, GU:WC], first)

            def tail(l):
                j, k, N = l + 1, BK[l] + 1, U[l]
                groups = last_groups(N)

                def up(i, between=None):
                    g, n, h = groups[i]
                    gate_up(l, g, g % 2, n % 2, h, between=between)

                def down_last(i):
                    g, n, h = groups[i]
                    s = n % 2
                    down(j, g, s, h, w_hi[:, s, GU:WC], w_lo[:, s, GU:WC], last=(n == N - 1))

                pe.wait_ge(wgu_lo[l], N - 1)
                up(0)
                pe.wait_ge(wgu_lo[l], N)
                up(1)
                unit_down(l, N - 3, (N - 3) % 2)
                up(2)
                if k == 4:
                    up(3)
                pe.wait_ge(wdn_lo[l], N - 1)
                down_last(0)
                pe.wait_ge(wdn_lo[l], N)
                down_last(1)
                if k < 4:
                    up(3, between=lambda: turn_sums(k, 0))
                down_last(2)
                if k < 4:
                    keep_clock(10)
                else:
                    turn_sums(k, 0)
                down_last(3)
                if k < 4:
                    turn_norm(k, 0)
                turn_sums(k, 1)

            def logits(h):
                pe.wait_ge(hT_done[1], 2 * h + 2)
                for t in range(TH):
                    for c in range(C):
                        at = HW * h + P * t
                        mm = pe.matmul(y_bank(1, h)[:, E[0] * t:E[0] * t + E[0]], hT[:, c, at:at + P],
                                       gate[0][:, c, :], start=(c == 0), stop=(c == C - 1))
                mm.then_inc(logits_done[0], 1)

            def logits1(h):
                pe.wait_ge(hT_done[3], 2 * h + 2)
                for t in range(TH):
                    for c in range(C):
                        at = HW * h + P * t
                        mm = pe.matmul(y_bank(1, h)[:, E[1] * t:E[1] * t + E[1]], hT[:, c, at:at + P],
                                       gate[1][:, c, :], start=(c == 0), stop=(c == C - 1))
                mm.then_inc(logits_done[1], 1)

            def hidden(g):
                n, h = g % NA, g // NA
                e, f = n // FC, n % FC
                if h == 0 and f == 0:
                    pe.wait_ge(ctx_lo_done, e + 1)
                if g >= 4:
                    pe.wait_ge(prod_done[0], g - 3)
                for c in range(C):
                    if n == 0:
                        pe.wait_ge(lo_done[0], 2 * h + c + 1)
                    w = slice(P * f, P * f + P)
                    mm = split_product(ps[:, g % 4, :], ctxT_hi[:, e, c, w], ctxT_lo[:, e, c, w],
                                       hT_hi[:, c, half(h)], hT_lo[:, c, half(h)], c == 0, c == C - 1)
                mm.then_inc(gu_done[0], 1)

            def down_a(g):
                n, h = g % NA, g // NA
                e, f = n // FC, n % FC
                down(0, g, g // 2 % 2, h, ctxT_hi[:, e, f, :], ctxT_lo[:, e, f, :], n == 0, n == NA - 1,
                     place=g % 2)

            def down_0(g, n, h):
                pe.wait_ge(wdn_lo[0], n + 1)
                if n == 0:
                    pe.wait_ge(scores_done[0], h + 1)
                down(1, g, n, h, w_hi[:, n, GU:WC], w_lo[:, n, GU:WC], n == 0)

            pe.wait_ge(ident_ready, 1)
            keep_clock(11)
            turn_norm(0, 0)
            keep_clock(5)
            hidden(0)
            hidden(1)
            turn_norm(0, 1)
            hidden(2)
            hidden(3)
            for g in range(2 * NA):
                if g + 4 < 2 * NA:
                    hidden(g + 4)
                if g == NA + 1:
                    turn_sums(1, 0)
                if g == NA + 3:
                    turn_norm(1, 0)
                down_a(g)
            pe.wait_ge(gates_loaded, 32)
            logits(0)
            pe.wait_ge(wgu_lo[0], 1)
            pe.wait_ge(lo_done[1], 2)
            gate_up(0, 0, 0, 0, 0, before=None, between=lambda: turn_sums(1, 1))
            pe.wait_ge(wgu_lo[0], 2)
            gate_up(0, 1, 1, 1, 0, before=None)
            down_0(0, 0, 0)
            turn_norm(1, 1)
            down_0(1, 1, 0)
            logits(1)
            pe.wait_ge(lo_done[1], 4)
            gate_up(0, 2, 0, 0, 1, "shared")
            gate_up(0, 3, 1, 1, 1, "shared")
            pe.wait_ge(wgu_lo[0], 3)
            gate_up(0, 4, 0, 0, 0, "shared")
            down_0(2, 0, 1)
            down_0(3, 1, 1)
            gate_up(0, 5, 1, 0, 1, "shared")
            unit_up(0, 3, 1)
            unit_down(0, 2, 0)
            with pe.Fori(2, U[0] // 2 - 1) as q:
                for s in range(2):
                    unit_up(0, 2 * q + s, s)
                    unit_down(0, 2 * q - 1 + s, 1 - s)
            tail(0)
            pe.wait_ge(ctx_loaded, 16)

            def score(t):
                pe.wait_ge(hT_done[2], 2 * (t // TH) + 2)
                if t >= 2:
                    pe.wait_ge(sc_done, t - 1)
                for c in range(C):
                    mm = pe.matmul(ps[:, t % 2, 0:M], hT[:, c, P * t:P * t + P], ctxT_sb[:, t // 2, c, :],
                                   start=(c == 0), stop=(c == C - 1))
                mm.then_inc(s_done, 1)

            def turn_exp(t):
                pe.wait_ge(e_done, t + 1)
                if t >= 2:
                    pe.wait_ge(eT_copied, t - 1)
                for c in range(FC):
                    mm = pe.transpose(ps[:, 2 + t % 2, P * c:P * c + P], ex[:, t, P * c:P * c + P], ident[:, :])
                mm.then_inc(eT_done, 1)

            def readout(t):
                pe.wait_ge(eT_copied, t + 1)
                if t % TH == 0:
                    pe.wait_ge(hT_done[2], 2 * (t // TH) + 2)
                if t % TH >= 2:
                    pe.wait_ge(x_new[3], t - 1)
                for c in range(FC):
                    mm = pe.matmul(y_bank(t % 2, t // TH)[:, 0:D], exT[:, t, c, :], ctx_sb[:, t // 2, c, :],
                                   start=(c == 0), stop=(c == FC - 1))
                mm.then_inc(pv_done, 1)

            score(0)
            score(1)
            for t in range(2, NT + 3):
                if t < NT:
                    score(t)
                if t - 2 < NT and t >= 2:
                    turn_exp(t - 2)
                if t == 2:
                    turn_norm(2, 1)
                if t >= 3:
                    readout(t - 3)
                if t == NT:
                    turn_norm(3, 0)
            logits1(0)
            pe.wait_ge(wgu_lo[1], 1)
            pe.wait_ge(lo_done[3], 2)
            gate_up(1, 0, 0, 0, 0, before=None, between=lambda: turn_norm(3, 1))
            logits1(1)
            pe.wait_ge(lo_done[3], 4)
            gate_up(1, 1, 1, 0, 1, before=None)
            unit_up(1, 1, 1, "shared")
            pe.wait_ge(scores_done[1], 2)
            unit_down(1, 0, 0, first=True)
            with pe.Fori(1, (U[1] - 2) // 2) as q:
                for s in range(2):
                    unit_up(1, 2 * q + s, s)
                    unit_down(1, 2 * q - 1 + s, 1 - s)
            unit_up(1, U[1] - 3, 0)
            unit_down(1, U[1] - 4, 1)
            tail(1)


def kernel(x, itok_BxS_13_99985, ctx_2048, mask_BxS2_bk0, L0_ffn_gate_w, L0_ffn_w11, L0_ffn_w33, L0_ffn_w22,
           L0_ffn_sw1, L0_ffn_sw2, L0_ffn_sw3, L1_ffn_router_w, L1_ffn_gate_up_w, L1_ffn_down_w,
           L1_ffn_shared_gate_w, L1_ffn_shared_up_w, L1_ffn_shared_down_w):
    import numpy as np
    import concourse.bacc as bacc
    from concourse.bass_utils import run_bass_kernel_spmd

    def by_feature(w):
        u, d, i = w.shape
        return w.reshape(u, d // P, P, i).transpose(0, 2, 1, 3).reshape(u, P, d // P * i)

    def units(gate, up, down):
        return np.ascontiguousarray(np.concatenate([by_feature(gate), by_feature(up), down], axis=2))

    def hidden_units(w):
        return w.reshape(-1, P, w.shape[1]).transpose(0, 2, 1)

    a = {
        "x": x, "itok_BxS_13_99985": itok_BxS_13_99985, "ctx_2048": ctx_2048, "mask_BxS2_bk0": mask_BxS2_bk0,
        "L0_ffn_gate_w": L0_ffn_gate_w, "L0_ffn_w11": L0_ffn_w11, "L0_ffn_w33": L0_ffn_w33,
        "L0_ffn_w22": L0_ffn_w22, "L0_ffn_sw1": L0_ffn_sw1, "L0_ffn_sw2": L0_ffn_sw2, "L0_ffn_sw3": L0_ffn_sw3,
        "L1_ffn_router_w": L1_ffn_router_w, "L1_ffn_gate_up_w": L1_ffn_gate_up_w, "L1_ffn_down_w": L1_ffn_down_w,
        "L1_ffn_shared_gate_w": L1_ffn_shared_gate_w, "L1_ffn_shared_up_w": L1_ffn_shared_up_w,
        "L1_ffn_shared_down_w": L1_ffn_shared_down_w,
    }
    a = {k: np.asarray(v) for k, v in a.items()}
    w0 = units(np.concatenate([hidden_units(a["L0_ffn_sw1"]), a["L0_ffn_w11"].transpose(0, 2, 1)]),
               np.concatenate([hidden_units(a["L0_ffn_sw3"]), a["L0_ffn_w33"].transpose(0, 2, 1)]),
               np.concatenate([a["L0_ffn_sw2"].T.reshape(-1, P, a["L0_ffn_sw2"].shape[0]),
                               a["L0_ffn_w22"].transpose(0, 2, 1)]))
    gu, hid = a["L1_ffn_gate_up_w"], a["L1_ffn_gate_up_w"].shape[2] // 2
    w1 = units(np.concatenate([a["L1_ffn_shared_gate_w"][None], gu[:, :, :hid]]),
               np.concatenate([a["L1_ffn_shared_up_w"][None], gu[:, :, hid:]]),
               np.concatenate([a["L1_ffn_shared_down_w"][None], a["L1_ffn_down_w"]]))
    arrays = {
        "x": a["x"],
        "tok": a["itok_BxS_13_99985"].reshape(-1),
        "ctx": a["ctx_2048"],
        "ctxT": a["ctx_2048"].transpose(0, 2, 1),
        "mask": a["mask_BxS2_bk0"].view(np.int32),
        "gate0": a["L0_ffn_gate_w"].T.reshape(-1, P, a["L0_ffn_gate_w"].shape[0]).transpose(1, 0, 2),
        "w0": w0,
        "gate1": a["L1_ffn_router_w"].reshape(-1, P, a["L1_ffn_router_w"].shape[1]).transpose(1, 0, 2),
        "w1": w1,
    }
    arrays = {f"{k}_dram": np.ascontiguousarray(v) for k, v in arrays.items()}
    nc = bacc.Bacc("TRN2", target_bir_lowering=False, num_devices=1)
    args = [nc.dram_tensor(k, v.shape, mybir.dt.from_np(v.dtype), kind="ExternalInput").ap()
            for k, v in arrays.items()]
    out = nc.dram_tensor("out_dram", a["x"].shape, F32, kind="ExternalOutput").ap()
    block_kernel(nc, *args, out)
    r = run_bass_kernel_spmd(nc, [arrays], core_ids=[0])
    return r.results[0]["out_dram"]
```
